# Optimizing a Trainium2 kernel written in Bass

```python
import numpy as np
import jax
import jax.numpy as jnp

def _softmax(x, axis=-1):
    return jax.nn.softmax(x, axis=axis)

def _gelu(x):
    return jax.nn.gelu(x, approximate=True)

def _silu(x):
    return jax.nn.silu(x)

def _sigmoid(x):
    return jax.nn.sigmoid(x)

def _layernorm(x, axis=-1, eps=1e-05):
    m = jnp.mean(x, axis=axis, keepdims=True)
    v = jnp.var(x, axis=axis, keepdims=True)
    return (x - m) / jnp.sqrt(v + eps)

def _scatter_add(tgt, idx, src, axis=0):
    return tgt.at[idx].add(src)

def _segment_sum(src, seg, n):
    return jax.ops.segment_sum(src, seg, n)
kernel_name = 'mk_macaron_d1_jaxref_r4_c3013c'

def setup_inputs(seed: int=0):
    np.random.seed(seed)
    _w = jnp.asarray

    def _L0_attn_setup():
        import jax, jax.numpy as jnp
        import numpy as np
        B, L, D, N, K = (4, 1024, 256, 64, 3)
        EPS = 1e-06

        def _ssm(x, win, wout, logA, Bp, Cp, logdt):
            dt = jnp.exp(logdt)
            A = -jnp.exp(logA)
            Abar = jnp.exp(A * dt)
            denom = jnp.where(jnp.abs(A) < EPS, jnp.ones_like(A), A)
            frac = jnp.where(jnp.abs(A) < EPS, dt, (Abar - 1.0) / denom)
            Bbar = frac * Bp
            u = jnp.einsum('bld,nd->bln', x, win)
            h0 = jnp.zeros((x.shape[0], win.shape[0]), x.dtype)

            def step(h, ut):
                h = h * Abar + ut * Bbar
                return (h, h * Cp)
            _, ys = jax.lax.scan(step, h0, jnp.swapaxes(u, 0, 1))
            y = jnp.swapaxes(ys, 0, 1)
            return jnp.einsum('bln,dn->bld', y, wout)
        key = jax.random.key(seed)
        ks = jax.random.split(key, 24)
        f32 = jnp.float32
        inp = {'T': jax.random.normal(ks[0], (B, L, D), f32), 'norm_scale': jnp.ones((D,), f32), 'in_w': jax.random.normal(ks[1], (2 * D, D), f32) * (1.0 / np.sqrt(D)), 'in_b': jnp.zeros((2 * D,), f32), 'dw_w': jax.random.normal(ks[2], (D, 1, K), f32) * (1.0 / np.sqrt(K)), 'dw_b': jnp.zeros((D,), f32), 'pw_w': jax.random.normal(ks[3], (D, D), f32) * (1.0 / np.sqrt(D)), 'pw_b': jnp.zeros((D,), f32), 'f_win': jax.random.normal(ks[4], (N, D), f32) * (1.0 / np.sqrt(D)), 'f_wout': jax.random.normal(ks[5], (D, N), f32) * (1.0 / np.sqrt(N)), 'f_logA': jax.random.normal(ks[6], (N,), f32) * 0.02, 'f_B': jax.random.normal(ks[7], (N,), f32) * 0.02, 'f_C': jax.random.normal(ks[8], (N,), f32) * 0.02, 'f_logdt': jnp.array(0.0, f32), 'b_win': jax.random.normal(ks[9], (N, D), f32) * (1.0 / np.sqrt(D)), 'b_wout': jax.random.normal(ks[10], (D, N), f32) * (1.0 / np.sqrt(N)), 'b_logA': jax.random.normal(ks[11], (N,), f32) * 0.02, 'b_B': jax.random.normal(ks[12], (N,), f32) * 0.02, 'b_C': jax.random.normal(ks[13], (N,), f32) * 0.02, 'b_logdt': jnp.array(0.0, f32), 'out_w': jax.random.normal(ks[14], (D, D), f32) * (1.0 / np.sqrt(D)), 'out_b': jnp.zeros((D,), f32)}
        return inp
    _L0_attn_in = _L0_attn_setup()

    def _L0_ffn_setup():
        import jax, jax.numpy as jnp
        import numpy as np
        B, S, H, I, E, K = (2, 512, 256, 512, 8, 2)
        key = jax.random.key(seed)
        k1, k2, k3, k4, k5 = jax.random.split(key, 5)
        scale_h = 1.0 / np.sqrt(H)
        scale_i = 1.0 / np.sqrt(I)
        return {'x': jax.random.normal(k1, (B, S, H), dtype=jnp.float32), 'Wg': jax.random.normal(k2, (H, E), dtype=jnp.float32) * scale_h, 'W11': jax.random.normal(k3, (E, H, I), dtype=jnp.float32) * scale_h, 'W12': jax.random.normal(k4, (E, H, I), dtype=jnp.float32) * scale_h, 'W2': jax.random.normal(k5, (E, I, H), dtype=jnp.float32) * scale_i}
    _L0_ffn_in = _L0_ffn_setup()
    _d = {'L0_attn_T': _L0_attn_in['T'], 'L0_attn_norm_scale': _L0_attn_in['norm_scale'], 'L0_attn_in_w': _L0_attn_in['in_w'], 'L0_attn_in_b': _L0_attn_in['in_b'], 'L0_attn_dw_w': _L0_attn_in['dw_w'], 'L0_attn_dw_b': _L0_attn_in['dw_b'], 'L0_attn_pw_w': _L0_attn_in['pw_w'], 'L0_attn_pw_b': _L0_attn_in['pw_b'], 'L0_attn_f_win': _L0_attn_in['f_win'], 'L0_attn_f_wout': _L0_attn_in['f_wout'], 'L0_attn_f_logA': _L0_attn_in['f_logA'], 'L0_attn_f_B': _L0_attn_in['f_B'], 'L0_attn_f_C': _L0_attn_in['f_C'], 'L0_attn_f_logdt': _L0_attn_in['f_logdt'], 'L0_attn_b_win': _L0_attn_in['b_win'], 'L0_attn_b_wout': _L0_attn_in['b_wout'], 'L0_attn_b_logA': _L0_attn_in['b_logA'], 'L0_attn_b_B': _L0_attn_in['b_B'], 'L0_attn_b_C': _L0_attn_in['b_C'], 'L0_attn_b_logdt': _L0_attn_in['b_logdt'], 'L0_attn_out_w': _L0_attn_in['out_w'], 'L0_attn_out_b': _L0_attn_in['out_b'], 'L0_ffn_Wg': _L0_ffn_in['Wg'], 'L0_ffn_W11': _L0_ffn_in['W11'], 'L0_ffn_W12': _L0_ffn_in['W12'], 'L0_ffn_W2': _L0_ffn_in['W2']}
    _x0 = _d['L0_attn_T']
    _d['L0_attn_T'] = jax.random.normal(jax.random.fold_in(jax.random.key(seed), 1), (1, 4096, 256), dtype=_x0.dtype)
    del _x0
    return _d

def reference(L0_attn_T, L0_attn_norm_scale, L0_attn_in_w, L0_attn_in_b, L0_attn_dw_w, L0_attn_dw_b, L0_attn_pw_w, L0_attn_pw_b, L0_attn_f_win, L0_attn_f_wout, L0_attn_f_logA, L0_attn_f_B, L0_attn_f_C, L0_attn_f_logdt, L0_attn_b_win, L0_attn_b_wout, L0_attn_b_logA, L0_attn_b_B, L0_attn_b_C, L0_attn_b_logdt, L0_attn_out_w, L0_attn_out_b, L0_ffn_Wg, L0_ffn_W11, L0_ffn_W12, L0_ffn_W2):

    def _L0_attn_ref(T, norm_scale, in_w, in_b, dw_w, dw_b, pw_w, pw_b, f_win, f_wout, f_logA, f_B, f_C, f_logdt, b_win, b_wout, b_logA, b_B, b_C, b_logdt, out_w, out_b):
        import jax, jax.numpy as jnp
        import numpy as np
        B, L, D, N, K = (4, 1024, 256, 64, 3)
        EPS = 1e-06

        def _ssm(x, win, wout, logA, Bp, Cp, logdt):
            dt = jnp.exp(logdt)
            A = -jnp.exp(logA)
            Abar = jnp.exp(A * dt)
            denom = jnp.where(jnp.abs(A) < EPS, jnp.ones_like(A), A)
            frac = jnp.where(jnp.abs(A) < EPS, dt, (Abar - 1.0) / denom)
            Bbar = frac * Bp
            u = jnp.einsum('bld,nd->bln', x, win)
            h0 = jnp.zeros((x.shape[0], win.shape[0]), x.dtype)

            def step(h, ut):
                h = h * Abar + ut * Bbar
                return (h, h * Cp)
            _, ys = jax.lax.scan(step, h0, jnp.swapaxes(u, 0, 1))
            y = jnp.swapaxes(ys, 0, 1)
            return jnp.einsum('bln,dn->bld', y, wout)
        rms = jnp.sqrt(jnp.mean(T * T, axis=-1, keepdims=True) + EPS)
        Tn = T / rms * norm_scale
        xz = Tn @ in_w.T + in_b
        x, z = jnp.split(xz, 2, axis=-1)
        gate = jax.nn.sigmoid(z)
        xc = jnp.swapaxes(x, 1, 2)
        xc = jax.lax.conv_general_dilated(xc, dw_w, window_strides=(1,), padding=[(K // 2, K // 2)], dimension_numbers=('NCH', 'OIH', 'NCH'), feature_group_count=D)
        xc = xc + dw_b[None, :, None]
        xc = jnp.einsum('bdl,ed->bel', xc, pw_w) + pw_b[None, :, None]
        x_conv = jnp.swapaxes(xc, 1, 2)
        y_f = _ssm(x_conv, f_win, f_wout, f_logA, f_B, f_C, f_logdt)
        y_b = _ssm(jnp.flip(x_conv, axis=1), b_win, b_wout, b_logA, b_B, b_C, b_logdt)
        y_b = jnp.flip(y_b, axis=1)
        y = (y_f + y_b) * gate
        y = y @ out_w.T + out_b
        return T + y

    def _L0_ffn_ref(x, Wg, W11, W12, W2):
        import jax, jax.numpy as jnp
        import numpy as np
        B, S, H, I, E, K = (2, 512, 256, 512, 8, 2)
        gate_scores = jax.nn.softmax(x @ Wg, axis=-1)
        topk_scores, topk_idx = jax.lax.top_k(gate_scores, K)
        topk_scores = topk_scores / (topk_scores.sum(-1, keepdims=True) + 1e-08)
        gate = jnp.einsum('bsh,ehi->bsei', x, W11)
        value = jnp.einsum('bsh,ehi->bsei', x, W12)
        fused = gate * jax.nn.sigmoid(gate) * value
        expert_out = jnp.einsum('bsei,eih->bseh', fused, W2)
        gathered = jnp.take_along_axis(expert_out, topk_idx[..., None], axis=2)
        out = jnp.sum(topk_scores[..., None] * gathered, axis=2)
        return out
    x = L0_attn_T
    x = x + 0.5 * _L0_ffn_ref(_layernorm(x, axis=-1), L0_ffn_Wg, L0_ffn_W11, L0_ffn_W12, L0_ffn_W2)
    x = x + _L0_attn_ref(_layernorm(x, axis=-1), L0_attn_norm_scale, L0_attn_in_w, L0_attn_in_b, L0_attn_dw_w, L0_attn_dw_b, L0_attn_pw_w, L0_attn_pw_b, L0_attn_f_win, L0_attn_f_wout, L0_attn_f_logA, L0_attn_f_B, L0_attn_f_C, L0_attn_f_logdt, L0_attn_b_win, L0_attn_b_wout, L0_attn_b_logA, L0_attn_b_B, L0_attn_b_C, L0_attn_b_logdt, L0_attn_out_w, L0_attn_out_b)
    x = x + 0.5 * _L0_ffn_ref(_layernorm(x, axis=-1), L0_ffn_Wg, L0_ffn_W11, L0_ffn_W12, L0_ffn_W2)
    return x

_drawn_inputs = setup_inputs


def setup_inputs(seed=0):
    import zlib

    import numpy as np

    out = dict(_drawn_inputs(seed))
    spreads = {'L0_attn_norm_scale': (1.0, 0.2),
     'L0_attn_in_b': (0.0, 0.1),
     'L0_attn_dw_b': (0.0, 0.1),
     'L0_attn_pw_b': (0.0, 0.1),
     'L0_attn_out_b': (0.0, 0.1)}
    factors = {}
    for name, (base, spread) in spreads.items():
        noise = np.random.default_rng([zlib.crc32(name.encode()), seed]).standard_normal(out[name].shape)
        drawn = base * np.exp(spread * noise) if base else spread * noise
        out[name] = jnp.asarray(drawn.astype(out[name].dtype))
    for name, factor in factors.items():
        out[name] = (out[name] * factor).astype(out[name].dtype)
    return out
```

```python
from contextlib import ExitStack

import concourse.bass as bass
from concourse import mybir

F32 = mybir.dt.float32
I32 = mybir.dt.int32
U32 = mybir.dt.uint32
ALU = mybir.AluOpType
ACT = mybir.ActivationFunctionType
AX = mybir.AxisListType

P = 128
L, D = 4096, 256
E, I, TOPK = 8, 512, 2
N = 64
DC, IC = D // P, I // P
NT = L // P
G = 4
CH = G * P
NCH = NT // G
ET = L * TOPK // P + E - 1
NQ = NT * TOPK
QB = 4
NQB = NQ // QB
ROWS = L + P
LN_EPS, RMS_EPS, SUM_EPS, A_EPS = 1e-5, 1e-6, 1e-8, 1e-6

C_NS, C_INB, C_DWW, C_DWB, C_PWB, C_LOGA, C_B, C_C, C_LOGDT = 0, 2, 6, 12, 14, 16, 17, 18, 19
NCOLS = 20


def build(nc, x, wg, w11, w12, w2, in_wt, pw, wint, woutt, out_wt, out_b, cols, out):
    ctx = ExitStack()
    with ctx:
        def sb(name, shape, dt=F32):
            return ctx.enter_context(nc.sbuf_tensor(name, shape, dt))

        def sem(name):
            return ctx.enter_context(nc.semaphore(name))

        xn_dram = nc.dram_tensor("xn_rows", [ROWS, D], F32, kind="Internal").ap()
        x1_dram = nc.dram_tensor("x1_rows", [ROWS, D], F32, kind="Internal").ap()

        w11_sb = sb("w11_sb", [P, E * DC, I])
        w12_sb = sb("w12_sb", [P, E * DC, I])
        w2_sb = sb("w2_sb", [P, E * IC, D])
        wg_sb = sb("wg_sb", [P, DC, E])
        inw_sb = sb("inw_sb", [P, DC, 2 * D])
        outw_sb = sb("outw_sb", [P, DC, D])
        wct_sb = sb("wct_sb", [P, DC, P])
        woc_sb = sb("woc_sb", [P, D])
        outb_sb = sb("outb_sb", [P, D])
        col = sb("col", [P, NCOLS])

        ident = sb("ident", [P, P])
        iota_row = sb("iota_row", [P, P])
        e_rank = sb("e_rank", [P, E])
        tok_id = sb("tok_id", [P, NT, TOPK])
        ln_eps, rms_eps = sb("ln_eps", [P, G]), sb("rms_eps", [P, G])
        neg_half = sb("neg_half", [P, G])
        pad_id = sb("pad_id", [P, 1])
        ssm = sb("ssm", [P, 12])
        a_mask = sb("a_mask", [P, 1], U32)
        ABAR, BBAR, UB, EXPA, DT, AA, ADT, DEN, RDEN, FRAC, ONE = range(11)

        seq = sb("seq", [P, DC, L + 2])
        gate = sb("gate", [P, DC, L])
        states = sb("states", [P, 2, CH])
        work = sb("work", [P, 7168])
        logits = sb("logits", [P, NT, E])
        idx_i = sb("idx_i", [P, ET], I32)
        w_slot = sb("w_slot", [P, ET])
        eid = sb("eid", [P, ET], I32)
        idx_g = [sb(f"idx_g{p}", [P, 1], I32) for p in range(2)]
        idx_s = sb("idx_s", [P, 1], I32)
        bnst = sb("bnst", [P, 2, G, 6])
        mv = sb("mv", [P, 2, G, 2])
        rstd = sb("rstd", [P, 2, G])
        ssq = sb("ssq", [P, 2, G])
        fence = sb("fence", [P, 1])
        rms = sb("rms", [P, 2, G])

        def part(at, *shape):
            n = 1
            for s in shape:
                n *= s
            v = work[:, at:at + n]
            if len(shape) == 2:
                v = v.rearrange("p (a b) -> p a b", b=shape[1])
            if len(shape) == 3:
                v = v.rearrange("p (a b c) -> p a b c", b=shape[1], c=shape[2])
            return v

        xin = [part(b * 1024, G, D) for b in range(2)]
        xn = [part(2048 + b * 1024, G, D) for b in range(2)]
        xnt = [part(4096 + b * 1024, DC, CH) for b in range(2)]
        mix = part(6144, DC, CH)
        R = [part(k * 256, NT * E) for k in range(10)]
        tok = [part(2560 + k * 64, NT, TOPK) for k in range(8)]
        small = part(3072, 256)
        ohb = [part(3328 + b * 512, QB, P) for b in range(2)]
        oha = [part(4352 + b * 568, QB, 2, ET) for b in range(2)]
        eqa = [part(5504 + b * 284, QB, ET) for b in range(2)]
        before = part(6144, P)
        ones = part(6272, P)
        seg = part(6400, E, NT)
        xg = [part(b * 256, D) for b in range(2)]
        xt = [part(512 + b * 256, DC, P) for b in range(2)]
        sg = [part(1024 + b * 512, I) for b in range(2)]
        fu = [part(2048 + b * 512, I) for b in range(2)]
        ft = [part(3072 + b * 512, IC, P) for b in range(2)]
        yb = [part(4096 + b * 256, D) for b in range(2)]
        pw_sb = part(0, DC, D)
        wint_sb = part(512, DC, P)
        woutt_sb = part(768, D)
        zeros = part(6656, D)
        iota_i = sb("iota_i", [P, P], I32)

        bank = [ctx.enter_context(nc.psum_tensor(f"bank{k}", [P, 512], F32)) for k in range(8)]
        ps_t = bank[0:2]
        ps_p = bank[2:6]
        ps_l = bank[6]
        ps_u = bank[7]
        ps_x, ps_f = bank[0], bank[1]
        ps_g, ps_v = bank[2:4], bank[4:6]

        s_cols, s_setw, s_wg, s_attw, s_expw = (sem(n) for n in ("s_cols", "s_setw", "s_wg", "s_attw", "s_expw"))
        s_outb = sem("s_outb")
        pool_const, const_ready = sem("pool_const"), sem("const_ready")
        ssm_exp, ssm_step, ssm_ready, wct_done, wct_ready = (sem(n) for n in ("ssm_exp", "ssm_step", "ssm_ready", "wct_done", "wct_ready"))
        pads_out, x1_init = sem("pads_out"), sem("x1_init")
        x_in = [sem(f"x_in{b}") for b in range(2)]
        x_out = [sem(f"x_out{b}") for b in range(2)]
        xn_out = [sem(f"xn_out{b}") for b in range(2)]
        ln_step, mv_ready, rstd_step, rstd_ready, norm_ready = (sem(n) for n in ("ln_step", "mv_ready", "rstd_step", "rstd_ready", "norm_ready"))
        tr_done, xnt_ready, logits_done, logits_copied = (sem(n) for n in ("tr_done", "xnt_ready", "logits_done", "logits_copied"))
        ssq_ready, rms_step, rms_ready, res_step, res_ready, tn_ready = (sem(n) for n in ("ssq_ready", "rms_step", "rms_ready", "res_step", "res_ready", "tn_ready"))
        proj_done, xz_ready, states_in = sem("proj_done"), sem("xz_ready"), sem("states_in")
        conv_step, conv_ready, u_done, u_ready, fwd_done = (sem(n) for n in ("conv_step", "conv_ready", "u_done", "u_ready", "fwd_done"))
        bwd_done, y_done, yg_ready, o_done, x2_ready = (sem(n) for n in ("bwd_done", "y_done", "yg_ready", "o_done", "x2_ready"))
        route_step, route_exp, ranks_done, route_const, oh_step, oh_ready, inv_used, inv_done, slots_ready = (
            sem(n) for n in ("route_step", "route_exp", "ranks_done", "route_const", "oh_step", "oh_ready", "inv_used", "inv_done", "slots_ready"))
        score_ready = sem("score_ready")
        gather_idx, scatter_idx = sem("gather_idx"), sem("scatter_idx")
        xg_in = [sem(f"xg_in{p}") for p in range(2)]
        xg_tr, xt_ready, g_done, v_done, sg_ready, f_step, f_ready = (sem(n) for n in ("xg_tr", "xt_ready", "g_done", "v_done", "sg_ready", "f_step", "f_ready"))
        f_tr, ft_ready, ye_done, ye_ready, added = (sem(n) for n in ("f_tr", "ft_ready", "ye_done", "ye_ready", "added"))

        block = ctx.enter_context(nc.Block())

        def rows(dram, c):
            return dram[bass.ds(c * CH, CH), :].rearrange("(j p) d -> p j d", p=P)

        def tile_plan(eng, tile):
            tile(0, 0, 0, True, False)
            with eng.Fori(0, (ET - 3) // 2) as h:
                tile(h * 2 + 1, h, 1, False, False)
                tile(h * 2 + 2, h + 1, 0, False, False)
            tile(ET - 2, (ET - 2) // 2, 1, False, False)
            tile(ET - 1, (ET - 1) // 2, 0, False, True)

        RS = 40
        PAR = [(ET + 1) // 2, ET // 2]

        @block.sync
        def _(sp):
            sp.dma_start(col[:], cols).then_inc(s_cols, 16)
            sp.dma_start(wg_sb[:], wg.rearrange("(c p) e -> p c e", p=P)).then_inc(s_wg, 16)
            sp.dma_start(pw_sb, pw.rearrange("(c p) d -> p c d", p=P)).then_inc(s_setw, 16)
            sp.dma_start(wint_sb, wint.rearrange("(c p) n -> p c n", p=P)).then_inc(s_setw, 16)
            sp.dma_start(woutt_sb, woutt).then_inc(s_setw, 16)
            sp.wait_ge(const_ready, 1)
            for dram in (xn_dram, x1_dram, out):
                sp.dma_start(dram[L:ROWS, :], zeros).then_inc(pads_out, 16)
            sp.wait_ge(wct_ready, 1)

            for b in range(2):
                sp.dma_start(xin[b], rows(x, b)).then_inc(x_in[b], 16)
            with sp.Fori(0, NCH // 2 - 1) as j:
                for b in range(2):
                    sp.wait_ge(norm_ready, j * 2 + b + 1)
                    sp.dma_start(rows(xn_dram, j * 2 + b), xn[b]).then_inc(xn_out[b], 16)
                    sp.dma_start(xin[b], rows(x, j * 2 + b + 2)).then_inc(x_in[b], 16)
            for b in range(2):
                sp.wait_ge(norm_ready, NCH - 1 + b)
                sp.dma_start(rows(xn_dram, NCH - 2 + b), xn[b]).then_inc(xn_out[b], 16)
            sp.dma_start(x1_dram[0:L, :].rearrange("(p j) d -> p j d", p=P), x.rearrange("(p j) d -> p j d", p=P)).then_inc(x1_init, 16)

            sp.wait_ge(added, 16 * ET)
            for b in range(2):
                sp.dma_start(xin[b], rows(x1_dram, b)).then_inc(x_in[b], 16)
            with sp.Fori(0, NCH // 2 - 1) as j:
                for b in range(2):
                    sp.wait_ge(res_ready, j * 2 + b + 1)
                    sp.dma_start(rows(out, j * 2 + b), xin[b]).then_inc(x_out[b], 16)
                    sp.wait_ge(norm_ready, NCH + j * 2 + b + 1)
                    sp.wait_ge(x_out[b], j * 16 + 16)
                    sp.dma_start(xin[b], rows(x1_dram, j * 2 + b + 2)).then_inc(x_in[b], 16)
            for b in range(2):
                sp.wait_ge(res_ready, NCH - 1 + b)
                sp.dma_start(rows(out, NCH - 2 + b), xin[b]).then_inc(x_out[b], 16)
            for b in range(2):
                sp.wait_ge(x_out[b], 16 * (NCH // 2))

            for b in range(2):
                sp.dma_start(xin[b], rows(out, NCH - 1 - b)).then_inc(x_in[b], 16)
            with sp.Fori(0, NCH // 2 - 1) as j:
                for b in range(2):
                    c = j * -2 + (NCH - 1 - b)
                    ahead = j * -2 + (NCH - 3 - b)
                    sp.wait_ge(x2_ready, j * 2 + b + 1)
                    sp.dma_start(rows(out, c), xin[b]).then_inc(x_out[b], 16)
                    sp.wait_ge(norm_ready, 2 * NCH + j * 2 + b + 1)
                    sp.dma_start(rows(xn_dram, c), xn[b]).then_inc(xn_out[b], 16)
                    sp.wait_ge(x_out[b], j * 16 + 16 * (NCH // 2 + 1))
                    sp.dma_start(xin[b], rows(out, ahead)).then_inc(x_in[b], 16)
            for b in range(2):
                sp.wait_ge(x2_ready, NCH - 1 + b)
                sp.dma_start(rows(out, 1 - b), xin[b]).then_inc(x_out[b], 16)
                sp.wait_ge(norm_ready, 3 * NCH - 1 + b)
                sp.dma_start(rows(xn_dram, 1 - b), xn[b]).then_inc(xn_out[b], 16)
            sp.wait_ge(pads_out, 48)
            for b in range(2):
                sp.wait_ge(x_out[b], 16 * NCH)
                sp.wait_ge(xn_out[b], 16 * NCH)
            sp.wait_ge(added, 2 * 16 * ET)

        @block.gpsimd
        def _(pool):
            step = 0
            def link(ins):
                nonlocal step
                step += 1
                ins.then_inc(pool_const, 1)
                pool.wait_ge(pool_const, step)

            nc.gpsimd.memset(zeros, 0.0)
            nc.gpsimd.memset(neg_half[:], -0.5)
            nc.gpsimd.memset(ln_eps[:], LN_EPS)
            nc.gpsimd.memset(rms_eps[:], RMS_EPS)
            nc.gpsimd.memset(ssm[:, ONE:ONE + 1], 1.0)
            link(nc.gpsimd.memset(ident[:], 0.0))
            nc.gpsimd.affine_select(out=ident[:], in_=ident[:], compare_op=ALU.not_equal, fill=1.0, base=0,
                                    pattern=[[-1, P]], channel_multiplier=1)
            link(nc.gpsimd.iota(iota_i[:], pattern=[[1, P]], base=0, channel_multiplier=0))
            link(nc.gpsimd.tensor_copy(iota_row[:], iota_i[:]))
            link(nc.gpsimd.iota(iota_i[:, 0:E], pattern=[[-1, E]], base=E, channel_multiplier=0))
            link(nc.gpsimd.tensor_copy(e_rank[:], iota_i[:, 0:E]))
            link(nc.gpsimd.iota(iota_i[:, 0:1], pattern=[[1, 1]], base=L + 1, channel_multiplier=1))
            link(nc.gpsimd.tensor_copy(pad_id[:], iota_i[:, 0:1]))
            link(nc.gpsimd.iota(iota_i[:, 0:NQ], pattern=[[P, NT], [0, TOPK]], base=1, channel_multiplier=1))
            nc.gpsimd.tensor_copy(tok_id[:].rearrange("p t k -> p (t k)"), iota_i[:, 0:NQ]).then_inc(const_ready, 1)

            pool.wait_ge(s_outb, 16)

            def rsqrt_ln(k, b):
                pool.wait_ge(mv_ready, k + 1)
                nc.gpsimd.tensor_tensor(rstd[:, b, :], mv[:, b, :, 1], ln_eps[:], ALU.add).then_inc(rstd_step, 1)
                pool.wait_ge(rstd_step, k + 1)
                nc.gpsimd.tensor_tensor(rstd[:, b, :], rstd[:, b, :], neg_half[:], ALU.pow).then_inc(rstd_ready, 1)

            def route_consts(r):
                pool.wait_ge(logits_copied, NCH * (r + 1))
                for b in range(2):
                    pool.wait_ge(xn_out[b], 16 * (NCH // 2) * (r + 1))
                    if r == 1:
                        pool.wait_ge(x_out[b], 16 * NCH)
                nc.gpsimd.memset(before, 1.0)
                nc.gpsimd.memset(ones, 1.0)
                link(nc.gpsimd.memset(seg, 1.0))
                nc.gpsimd.affine_select(out=before, in_=before, compare_op=ALU.is_gt, fill=0.0, base=0,
                                        pattern=[[1, P]], channel_multiplier=-1)
                nc.gpsimd.memset(seg[:, :, 0], 0.0).then_inc(route_const, 1)

            def experts(r):
                base = r * ET

                def tile(t, h, p, first, last, more=True):
                    done = t + (base + 1)
                    if more:
                        pool.wait_ge(xg_tr, done)
                        nc.gpsimd.tensor_copy(idx_g[p][:], idx_i[:, bass.ds(t + 2, 1)]).then_inc(gather_idx, 1)
                        pool.wait_ge(pads_out, 48)
                        pool.wait_ge(gather_idx, done)
                        nc.gpsimd.indirect_dma_start(xg[p], None, xn_dram, bass.IndirectOffsetOnAxis(ap=idx_g[p][:], axis=0)).then_inc(xg_in[p], 16)
                    if not (first and r == 0):
                        pool.wait_ge(added, t * 16 + 16 * base)
                    nc.gpsimd.tensor_copy(idx_s[:], idx_i[:, bass.ds(t, 1)]).then_inc(scatter_idx, 1)
                    dst = x1_dram if r == 0 else out
                    pool.wait_ge(pads_out, 48)
                    pool.wait_ge(scatter_idx, done)
                    pool.wait_ge(ye_ready, done)
                    nc.gpsimd.indirect_dma_start(dst, bass.IndirectOffsetOnAxis(ap=idx_s[:], axis=0), yb[p], None,
                                                 compute_op=ALU.add).then_inc(added, 16)

                pool.wait_ge(slots_ready, r + 1)
                for b in range(2):
                    pool.wait_ge(xn_out[b], 16 * (NCH // 2) * (r + 1))
                pool.wait_ge(pads_out, 48)
                if r == 0:
                    pool.wait_ge(x1_init, 16)
                else:
                    for b in range(2):
                        pool.wait_ge(x_out[b], 16 * NCH)
                for t in range(2):
                    copy = nc.gpsimd.tensor_copy(idx_g[t][:], idx_i[:, t:t + 1])
                    if r == 0:
                        link(copy)
                    else:
                        copy.then_inc(gather_idx, 1)
                        pool.wait_ge(gather_idx, base - 1 + t)
                    nc.gpsimd.indirect_dma_start(xg[t], None, xn_dram, bass.IndirectOffsetOnAxis(ap=idx_g[t][:], axis=0)).then_inc(xg_in[t], 16)
                tile(0, 0, 0, True, False)
                with pool.Fori(0, (ET - 3) // 2) as h:
                    tile(h * 2 + 1, h, 1, False, False)
                    tile(h * 2 + 2, h + 1, 0, False, False)
                tile(ET - 2, 0, 1, False, False, more=False)
                tile(ET - 1, 0, 0, False, True, more=False)

            with pool.Fori(0, NCH // 2) as j:
                for b in range(2):
                    rsqrt_ln(j * 2 + b, b)
            route_consts(0)
            experts(0)
            with pool.Fori(0, NCH // 2) as j:
                for b in range(2):
                    i = j * 2 + b
                    rsqrt_ln(i + NCH, b)
                    pool.wait_ge(norm_ready, i + (NCH + 1))
                    nc.gpsimd.tensor_tensor(xin[b], xin[b], xn[b], ALU.add).then_inc(res_step, 1)
                    pool.wait_ge(ssq_ready, i + 1)
                    nc.gpsimd.tensor_tensor(rms[:, b, :], ssq[:, b, :], rms_eps[:], ALU.add).then_inc(rms_step, 1)
                    pool.wait_ge(rms_step, i + 1)
                    nc.gpsimd.tensor_tensor(rms[:, b, :], rms[:, b, :], neg_half[:], ALU.pow).then_inc(rms_ready, 1)
                    pool.wait_ge(res_step, i + 1)
                    nc.gpsimd.tensor_tensor(xin[b], xin[b], outb_sb[:].unsqueeze(1).to_broadcast([P, G, D]), ALU.add).then_inc(res_ready, 1)
            with pool.Fori(0, NCH // 2) as j:
                for b in range(2):
                    rsqrt_ln(j * 2 + (b + 2 * NCH), b)
            route_consts(1)
            experts(1)

        @block.scalar
        def _(act):
            act.dma_start(outb_sb[:], out_b.to_broadcast([P, D])).then_inc(s_outb, 16)
            act.dma_start(inw_sb[:], in_wt.rearrange("(c p) n -> p c n", p=P)).then_inc(s_attw, 16)
            act.dma_start(outw_sb[:], out_wt.rearrange("(c p) n -> p c n", p=P)).then_inc(s_attw, 16)
            act.dma_start(w11_sb[:], w11.rearrange("e (c p) i -> p (e c) i", p=P)).then_inc(s_expw, 16)
            act.dma_start(w12_sb[:], w12.rearrange("e (c p) i -> p (e c) i", p=P)).then_inc(s_expw, 16)
            act.dma_start(w2_sb[:], w2.rearrange("e (c p) d -> p (e c) d", p=P)).then_inc(s_expw, 16)
            act.wait_ge(s_cols, 16)
            nc.scalar.activation(ssm[:, EXPA:EXPA + 1], col[:, C_LOGA:C_LOGA + 1], ACT.Exp).then_inc(ssm_exp, 1)
            nc.scalar.activation(ssm[:, DT:DT + 1], col[:, C_LOGDT:C_LOGDT + 1], ACT.Exp).then_inc(ssm_exp, 1)
            act.wait_ge(ssm_step, 2)
            nc.scalar.activation(ssm[:, ABAR:ABAR + 1], ssm[:, ADT:ADT + 1], ACT.Exp).then_inc(ssm_exp, 1)

            def route_chunk(k, n, b, c):
                act.wait_ge(tr_done, k + 1)
                if not (isinstance(n, int) and n < 2):
                    act.wait_ge(logits_done, n - 1)
                for h in range(DC):
                    last = nc.scalar.activation(xnt[b][:, h, :], ps_t[h][:], ACT.Copy)
                last.then_inc(xnt_ready, 1)
                act.wait_ge(logits_done, n + 1)
                nc.scalar.activation(logits[:, bass.ds(c * G, G), :].rearrange("p t e -> p (t e)"), ps_l[:, 0:G * E], ACT.Copy).then_inc(logits_copied, 1)

            def router_exp(r):
                act.wait_ge(route_step, r * RS + 2)
                nc.scalar.activation(R[1], R[0], ACT.Exp).then_inc(route_exp, 1)

            def experts(r):
                base = r * ET

                def finish(t, p, first_ring):
                    act.wait_ge(f_tr, t + (base + 1))
                    act.wait_ge(ye_done, t + (base - 1)) if not first_ring else None
                    nc.scalar.activation(ft[p].rearrange("p c k -> p (c k)"), ps_f[:], ACT.Copy).then_inc(ft_ready, 1)
                    act.wait_ge(ye_done, t + (base + 1))
                    act.wait_ge(added, t * 16 + 16 * (base - 1)) if not first_ring else None
                    nc.scalar.activation(yb[p], ps_u[:, 0:D], ACT.Copy, scale=w_slot[:, bass.ds(t, 1)]).then_inc(ye_ready, 1)

                def tile(t, h, p, first, last):
                    act.wait_ge(g_done, t + (base + 1))
                    if not first:
                        act.wait_ge(f_step, t + (base - 1)) if not (isinstance(t, int) and t < 2) else None
                    nc.scalar.activation(sg[p], ps_g[p][:], ACT.Sigmoid).then_inc(sg_ready, 1)
                    if not first:
                        finish(t - 1, 1 - p, False)

                act.wait_ge(slots_ready, r + 1)
                tile(0, 0, 0, True, False)
                act.wait_ge(g_done, base + 2)
                nc.scalar.activation(sg[1], ps_g[1][:], ACT.Sigmoid).then_inc(sg_ready, 1)
                finish(0, 0, True)
                act.wait_ge(g_done, base + 3)
                act.wait_ge(f_step, base + 1)
                nc.scalar.activation(sg[0], ps_g[0][:], ACT.Sigmoid).then_inc(sg_ready, 1)
                finish(1, 1, True)
                with act.Fori(0, (ET - 3) // 2) as h:
                    tile(h * 2 + 3, h, 1, False, False)
                    tile(h * 2 + 4, h, 0, False, False)
                finish(ET - 1, 0, False)

            act.wait_ge(wct_ready, 1)
            for b in range(2):
                route_chunk(b, b, b, b)
            with act.Fori(0, NCH // 2 - 1) as j:
                for b in range(2):
                    route_chunk(j * 2 + (b + 2), j * 2 + (b + 2), b, j * 2 + (b + 2))
            router_exp(0)
            experts(0)
            with act.Fori(0, NCH // 2) as j:
                for b in range(2):
                    i = j * 2 + b
                    act.wait_ge(norm_ready, i + (NCH + 1))
                    for t in range(G):
                        last = nc.scalar.activation(states[:].rearrange("p b n -> p (b n)")[:, t * D:(t + 1) * D], xn[b][:, t, :], ACT.Square, scale=D ** -0.5, accum_out=ssq[:, b, t:t + 1])
                    last.then_inc(ssq_ready, 1)
                    act.wait_ge(tr_done, i + (NCH + 1))
                    act.wait_ge(ssq_ready, i + 1)
                    for h in range(DC):
                        last = nc.scalar.activation(xnt[b][:, h, :], ps_t[h][:], ACT.Copy, scale=col[:, C_NS + h:C_NS + h + 1])
                    last.then_inc(xnt_ready, 1)
                    for jc in range(2 * DC):
                        act.wait_ge(proj_done, j * 8 + (4 * b + jc + 1))
                        if jc < DC:
                            nc.scalar.activation(seq[:, jc, bass.ds(i * CH + 1, CH)], ps_p[jc][:], ACT.Identity,
                                                 bias=col[:, C_INB + jc:C_INB + jc + 1]).then_inc(xz_ready, 1)
                        else:
                            nc.scalar.activation(gate[:, jc - DC, bass.ds(i * CH, CH)], ps_p[jc][:], ACT.Sigmoid,
                                                 bias=col[:, C_INB + jc:C_INB + jc + 1]).then_inc(xz_ready, 1)
            with act.Fori(0, NCH // 2) as j:
                for b in range(2):
                    route_chunk(j * 2 + (b + 2 * NCH), j * 2 + (b + NCH), b, j * -2 + (NCH - 1 - b))
            router_exp(1)
            experts(1)

        @block.vector
        def _(dve):
            def chain(sem_, start):
                at = [start]

                def link(ins, wait=True):
                    at[0] += 1
                    ins.then_inc(sem_, 1)
                    if wait:
                        dve.wait_ge(sem_, at[0])
                return link, at

            link, at = chain(ssm_step, 0)
            v = lambda k: ssm[:, k:k + 1]
            dve.wait_ge(const_ready, 1)
            dve.wait_ge(ssm_exp, 2)
            link(nc.vector.tensor_scalar(v(AA), v(EXPA), -1.0, None, ALU.mult))
            link(nc.vector.tensor_tensor(v(ADT), v(AA), v(DT), ALU.mult))
            nc.vector.tensor_scalar(a_mask[:], v(EXPA), A_EPS, None, ALU.is_lt)
            link(nc.vector.tensor_copy(v(DEN), v(AA)))
            link(nc.vector.copy_predicated(v(DEN), a_mask[:], v(ONE)))
            link(nc.vector.reciprocal(v(RDEN), v(DEN)))
            dve.wait_ge(ssm_exp, 3)
            link(nc.vector.tensor_scalar(v(FRAC), v(ABAR), -1.0, v(RDEN), ALU.add, ALU.mult))
            link(nc.vector.copy_predicated(v(FRAC), a_mask[:], v(DT)))
            link(nc.vector.tensor_tensor(v(BBAR), v(FRAC), col[:, C_B:C_B + 1], ALU.mult))
            dve.wait_ge(s_setw, 48)
            nc.vector.tensor_scalar(woc_sb[:], woutt_sb, col[:, C_C:C_C + 1], None, ALU.mult)
            dve.wait_ge(wct_done, 1)
            nc.vector.tensor_copy(wct_sb[:].rearrange("p c n -> p (c n)"), ps_p[0][:, 0:D])
            nc.vector.memset(seq[:, :, 0:1], 0.0)
            nc.vector.memset(seq[:, :, L + 1:L + 2], 0.0)
            nc.vector.tensor_copy(v(UB), ps_p[1][:, 0:1]).then_inc(wct_ready, 1)
            dve.wait_ge(wct_ready, 1)

            def layer_norm(k, b, tr):
                for t in range(G):
                    last = nc.vector.bn_stats(bnst[:, b, t, :], xin[b][:, t, :])
                last.then_inc(ln_step, 1)
                dve.wait_ge(ln_step, k + 1)
                nc.vector.memset(fence[:], 0.0)
                for t in range(G):
                    last = nc.vector.bn_aggr(mv[:, b, t, :], bnst[:, b, t, :])
                last.then_inc(mv_ready, 1)
                dve.wait_ge(mv_ready, k + 1)
                dve.wait_ge(rstd_ready, k + 1)
                if tr is not None:
                    dve.wait_ge(tr_done, tr)
                for t in range(G):
                    last = nc.vector.tensor_scalar(xn[b][:, t, :], xin[b][:, t, :], mv[:, b, t, 0:1], rstd[:, b, t:t + 1], ALU.subtract, ALU.mult)
                last.then_inc(norm_ready, 1)

            def router(r):
                link, at = chain(route_step, r * RS)
                grid = lambda a: a.rearrange("p (t e) -> p t e", e=E)
                cols_ = lambda a: a.rearrange("p (e t) -> p e t", e=E)
                flip = lambda a: a.rearrange("p (e t) -> p t e", e=E)
                over_e = lambda a: a.unsqueeze(2).to_broadcast([P, NT, E])
                rank = e_rank[:].unsqueeze(1).to_broadcast([P, NT, E])
                lg = logits[:]
                s0, s1, s2, s3 = (small[:, k * NT:(k + 1) * NT] for k in range(4))
                best = [tok[0][:, :, k] for k in range(TOPK)]
                dve.wait_ge(route_const, r + 1)
                link(nc.vector.reduce_max(s0, lg, AX.X))
                link(nc.vector.tensor_tensor(grid(R[0]), lg, over_e(s0), ALU.subtract))
                dve.wait_ge(route_exp, r + 1)
                link(nc.vector.reduce_sum(s1, grid(R[1]), AX.X))
                link(nc.vector.reciprocal(s2, s1))
                link(nc.vector.tensor_tensor(grid(R[2]), grid(R[1]), over_e(s2), ALU.mult))
                onehot = [R[5], R[8]]
                prob = R[2]
                for k in range(TOPK):
                    link(nc.vector.reduce_max(best[k], grid(prob), AX.X))
                    link(nc.vector.tensor_tensor(grid(R[3]), grid(prob), over_e(best[k]), ALU.is_equal))
                    link(nc.vector.tensor_tensor(grid(R[4]), grid(R[3]), rank, ALU.mult))
                    link(nc.vector.reduce_max(s3, grid(R[4]), AX.X))
                    link(nc.vector.tensor_tensor(flip(onehot[k]), over_e(s3), rank, ALU.is_equal))
                    if k == 0:
                        link(nc.vector.scalar_tensor_tensor(grid(R[6]), flip(onehot[0]), -2.0, grid(prob), ALU.mult, ALU.add))
                        prob = R[6]
                link(nc.vector.tensor_tensor(R[9], onehot[0], onehot[1], ALU.add))
                link(nc.vector.tensor_tensor(s0, best[0], best[1], ALU.add))
                link(nc.vector.tensor_scalar(s1, s0, SUM_EPS, None, ALU.add))
                link(nc.vector.reciprocal(s2, s1))
                for k in range(TOPK):
                    last = nc.vector.scalar_tensor_tensor(tok[1][:, :, k], best[k], 0.5, s2, ALU.mult, ALU.mult)
                link(last)
                cnt, tiles_i, tiles, ends, first = (small[:, 128 + 8 * k:136 + 8 * k] for k in range(5))
                dve.wait_ge(ranks_done, r + 1)
                rank_ps, tot_ps = ps_u[:, 0:NT * E], ps_u[:, NT * E:2 * NT * E]
                link(nc.vector.tensor_copy(R[0], tot_ps))
                nc.vector.reduce_sum(cnt, cols_(R[0]), AX.X)
                link(nc.vector.tensor_tensor_scan(R[1], seg.rearrange("p e t -> p (e t)"), R[0], 0.0, ALU.mult, ALU.add))
                link(nc.vector.tensor_scalar(tiles_i.bitcast(I32), cnt, float(P - 1), None, ALU.add))
                link(nc.vector.tensor_scalar(tiles_i.bitcast(I32), tiles_i.bitcast(I32), 7, None, ALU.logical_shift_right))
                link(nc.vector.tensor_copy(tiles, tiles_i.bitcast(I32)))
                link(nc.vector.tensor_tensor_scan(ends, ones[:, 0:E], tiles, 0.0, ALU.mult, ALU.add))
                link(nc.vector.tensor_tensor(first, ends, tiles, ALU.subtract))
                link(nc.vector.tensor_tensor(R[1], R[1], R[0], ALU.subtract))
                link(nc.vector.tensor_tensor(R[2], rank_ps, R[1], ALU.add))
                link(nc.vector.scalar_tensor_tensor(cols_(R[3]), first.unsqueeze(2).to_broadcast([P, E, NT]), float(P), cols_(R[2]), ALU.mult, ALU.add))
                for k in range(TOPK):
                    last = nc.vector.tensor_tensor([R[4], R[7]][k], onehot[k], R[3], ALU.mult)
                link(last)
                for k in range(TOPK):
                    last = nc.vector.reduce_sum(tok[2][:, :, k], flip([R[4], R[7]][k]), AX.X)
                link(last)
                ge = R[0][:, 0:(E - 1) * 32]
                flat = lambda a: a.rearrange("p t k -> p (t k)")
                link(nc.vector.tensor_copy(flat(tok[3]).bitcast(I32), flat(tok[2])))
                nc.vector.tensor_scalar(flat(tok[4]).bitcast(I32), flat(tok[3]).bitcast(I32), P - 1, None, ALU.bitwise_and)
                link(nc.vector.tensor_scalar(flat(tok[5]).bitcast(I32), flat(tok[3]).bitcast(I32), 7, None, ALU.logical_shift_right))
                nc.vector.tensor_copy(flat(tok[6]), flat(tok[4]).bitcast(I32))
                link(nc.vector.tensor_copy(flat(tok[7]), flat(tok[5]).bitcast(I32)))
                big = work[:, 0:ET * (E - 1)].rearrange("p (t e) -> p t e", e=E - 1)
                link(nc.vector.tensor_tensor(big, iota_row[:, 0:ET].unsqueeze(2).to_broadcast([P, ET, E - 1]),
                                             ends[:, 0:E - 1].unsqueeze(1).to_broadcast([P, ET, E - 1]), ALU.is_ge))
                link(nc.vector.reduce_sum(R[2][:, 0:ET], big, AX.X))
                link(nc.vector.tensor_copy(eid[:], R[2][:, 0:ET]))
                ob = r * NQB

                def onehots(s, b, free):
                    if free:
                        dve.wait_ge(inv_used, s + (ob - 1))
                    q = bass.ds(s * QB, QB)
                    place, tile_, ids, score = (flat(a)[:, q].unsqueeze(2) for a in (tok[6], tok[7], tok_id[:], tok[1]))
                    nc.vector.tensor_tensor(ohb[b], iota_row[:].unsqueeze(1).to_broadcast([P, QB, P]), place.to_broadcast([P, QB, P]), ALU.is_equal)
                    nc.vector.tensor_tensor(eqa[b], iota_row[:, 0:ET].unsqueeze(1).to_broadcast([P, QB, ET]), tile_.to_broadcast([P, QB, ET]), ALU.is_equal).then_inc(oh_step, 1)
                    dve.wait_ge(oh_step, s + (ob + 1))
                    nc.vector.tensor_tensor(oha[b][:, :, 0, :], eqa[b], ids.to_broadcast([P, QB, ET]), ALU.mult)
                    nc.vector.tensor_tensor(oha[b][:, :, 1, :], eqa[b], score.to_broadcast([P, QB, ET]), ALU.mult).then_inc(oh_ready, 1)

                onehots(0, 0, False)
                onehots(1, 1, False)
                with dve.Fori(0, NQB // 2 - 1) as j:
                    onehots(j * 2 + 2, 0, True)
                    onehots(j * 2 + 3, 1, True)
                dve.wait_ge(inv_done, r + 1)
                inv_id, inv_w = ps_l[:, 0:ET], ps_l[:, ET:2 * ET]
                nc.vector.tensor_copy(w_slot[:], inv_w)
                link(nc.vector.tensor_scalar(R[2][:, 0:ET], inv_id, 0.0, pad_id[:], ALU.is_equal, ALU.mult))
                nc.vector.scalar_tensor_tensor(idx_i[:], inv_id, -1.0, R[2][:, 0:ET], ALU.add, ALU.add).then_inc(slots_ready, 1)
                dve.wait_ge(slots_ready, r + 1)
                assert at[0] == (r + 1) * RS, at[0] - r * RS

            def experts(r):
                base = r * ET

                def rows_in(t, p):
                    dve.wait_ge(xg_tr, t + (base + 1))
                    nc.vector.tensor_copy(xt[p].rearrange("p c k -> p (c k)"), ps_x[:, 0:D]).then_inc(xt_ready, 1)

                def tile(t, h, p, first, last):
                    dve.wait_ge(sg_ready, t + (base + 1))
                    nc.vector.tensor_tensor(sg[p], sg[p], ps_g[p][:], ALU.mult).then_inc(f_step, 1)
                    dve.wait_ge(f_step, t + (base + 1))
                    dve.wait_ge(v_done, t + (base + 1))
                    nc.vector.tensor_tensor(fu[p], sg[p], ps_v[p][:], ALU.mult).then_inc(f_ready, 1)
                    if not last:
                        rows_in(t + 1, 1 - p)

                rows_in(0, 0)
                tile_plan(dve, tile)

            for b in range(2):
                dve.wait_ge(x_in[b], 16)
                layer_norm(b, b, None)
            with dve.Fori(0, NCH // 2 - 1) as j:
                for b in range(2):
                    dve.wait_ge(x_in[b], j * 16 + 32)
                    dve.wait_ge(xn_out[b], j * 16 + 16)
                    layer_norm(j * 2 + (b + 2), b, j * 2 + (b + 1))
            router(0)
            experts(0)

            def mixer_in(i, j, b):
                dve.wait_ge(x_in[b], j * 16 + 16 * (NCH // 2 + 1))
                layer_norm(i + NCH, b, i + (NCH - 1))
                dve.wait_ge(rms_ready, i + 1)
                dve.wait_ge(res_step, i + 1)
                dve.wait_ge(norm_ready, i + (NCH + 1))
                for t in range(G):
                    last = nc.vector.tensor_scalar(xn[b][:, t, :], xn[b][:, t, :], rms[:, b, t:t + 1], None, ALU.mult)
                last.then_inc(tn_ready, 1)

            def conv_scan(c, first):
                dww = lambda h, k: col[:, C_DWW + 3 * h + k:C_DWW + 3 * h + k + 1]
                last_c = isinstance(c, int) and c == NCH - 1
                dve.wait_ge(xz_ready, NCH * 4 if last_c else c * 4 + (4 + DC))
                if not first:
                    dve.wait_ge(u_done, c)
                for h in range(DC):
                    last = nc.vector.tensor_scalar(mix[:, h, :], seq[:, h, bass.ds(c * CH + 1, CH)], dww(h, 1), col[:, C_DWB + h:C_DWB + h + 1], ALU.mult, ALU.add)
                last.then_inc(conv_step, 1)
                dve.wait_ge(conv_step, c * 2 + 1)
                for h in range(DC):
                    last = nc.vector.scalar_tensor_tensor(mix[:, h, :], seq[:, h, bass.ds(c * CH, CH)], dww(h, 0), mix[:, h, :], ALU.mult, ALU.add)
                last.then_inc(conv_step, 1)
                dve.wait_ge(conv_step, c * 2 + 2)
                for h in range(DC):
                    last = nc.vector.scalar_tensor_tensor(mix[:, h, :], seq[:, h, bass.ds(c * CH + 2, CH)], dww(h, 2), mix[:, h, :], ALU.mult, ALU.add)
                last.then_inc(conv_ready, 1)
                dve.wait_ge(conv_ready, c + 1)
                dve.wait_ge(u_done, c + 1)
                nc.vector.tensor_scalar(seq[:, 0, bass.ds(c * CH, CH)], ps_u[:], v(UB), v(BBAR), ALU.add, ALU.mult).then_inc(u_ready, 1)
                dve.wait_ge(u_ready, c + 1)
                if not first:
                    dve.wait_ge(fwd_done, c)
                here = seq[0:N, 0, bass.ds(c * CH, CH)]
                nc.vector.tensor_tensor_scan(here, ssm[0:N, ABAR:ABAR + 1].to_broadcast([N, CH]), here,
                                             0.0 if first else seq[0:N, 0, bass.ds(c * CH - 1, 1)], ALU.mult, ALU.add).then_inc(fwd_done, 1)

            mixer_in(0, 0, 0)
            mixer_in(1, 0, 1)
            conv_scan(0, True)
            with dve.Fori(0, NCH // 2 - 1) as j:
                mixer_in(j * 2 + 2, j + 1, 0)
                conv_scan(j * 2 + 1, False)
                mixer_in(j * 2 + 3, j + 1, 1)
                conv_scan(j * 2 + 2, False)
            conv_scan(NCH - 1, False)
            dve.wait_ge(ssq_ready, NCH)
            nc.vector.memset(states[N:P, 1, 0:1], 0.0).then_inc(bwd_done, 1)
            dve.wait_ge(fwd_done, NCH)

            with dve.Fori(0, NCH // 2) as j:
                for b in range(2):
                    i, c = j * 2 + b, j * -2 + (NCH - 1 - b)
                    dve.wait_ge(bwd_done, i + 1)
                    nc.vector.tensor_copy(states[:, b, :], seq[:, 0, bass.ds(c * CH, CH)]).then_inc(states_in, 1)
                    dve.wait_ge(states_in, i + 1)
                    back = states[N:P, b, ::-1]
                    nc.vector.tensor_tensor_scan(back, ssm[N:P, ABAR:ABAR + 1].to_broadcast([N, CH]), back,
                                                 states[N:P, 1 - b, 0:1], ALU.mult, ALU.add).then_inc(bwd_done, 1)
                    dve.wait_ge(y_done, i + 1)
                    for h in range(DC):
                        last = nc.vector.tensor_tensor(mix[:, h, :], gate[:, h, bass.ds(c * CH, CH)], ps_p[h][:], ALU.mult)
                    last.then_inc(yg_ready, 1)
                    dve.wait_ge(x_in[b], j * 16 + 16 * (NCH + 1))
                    dve.wait_ge(o_done, i + 1)
                    for h in range(2):
                        last = nc.vector.tensor_tensor(xin[b][:, 2 * h:2 * h + 2, :].rearrange("p t d -> p (t d)"),
                                                       xin[b][:, 2 * h:2 * h + 2, :].rearrange("p t d -> p (t d)"), ps_p[2 + h][:], ALU.add)
                    last.then_inc(x2_ready, 1)
                    dve.wait_ge(x2_ready, i + 1)
                    dve.wait_ge(xn_out[b], j * 16 + 16 * (NCH // 2))
                    layer_norm(i + 2 * NCH, b, i + (2 * NCH - 1))
            router(1)
            experts(1)

        @block.tensor
        def _(pe):
            pe.wait_ge(const_ready, 1)
            pe.wait_ge(s_setw, 48)
            pe.wait_ge(s_cols, 16)
            for dc in range(DC):
                for ec in range(DC):
                    nc.tensor.matmul(ps_p[0][:, dc * P:(dc + 1) * P], pw_sb[:, ec, dc * P:(dc + 1) * P], wint_sb[:, ec, :],
                                     start=(ec == 0), stop=(ec == DC - 1))
            for ec in range(DC):
                last = nc.tensor.matmul(ps_p[1][:, 0:1], wint_sb[:, ec, :], col[:, C_PWB + ec:C_PWB + ec + 1], start=(ec == 0), stop=(ec == DC - 1))
            last.then_inc(wct_done, 1)
            pe.wait_ge(s_wg, 16)

            def transposes(b):
                for t in range(G):
                    for h in range(DC):
                        last = nc.tensor.transpose(ps_t[h][:, t * P:(t + 1) * P], xn[b][:, t, h * P:(h + 1) * P], ident[:])
                last.then_inc(tr_done, 1)

            def route_chunk(k, n, b, first):
                pe.wait_ge(norm_ready, k + 1)
                if not first:
                    pe.wait_ge(xnt_ready, k)
                transposes(b)
                pe.wait_ge(xnt_ready, k + 1)
                if not first:
                    pe.wait_ge(logits_copied, n)
                for t in range(G):
                    for h in range(DC):
                        last = nc.tensor.matmul(ps_l[:, t * E:(t + 1) * E], xnt[b][:, h, t * P:(t + 1) * P], wg_sb[:, h, :],
                                                start=(h == 0), stop=(h == DC - 1))
                last.then_inc(logits_done, 1)

            def router(r):
                pe.wait_ge(route_step, r * RS + 17)
                nc.tensor.matmul(ps_u[:, 0:NT * E], before, R[9], start=True, stop=True)
                nc.tensor.matmul(ps_u[:, NT * E:2 * NT * E], ones, R[9], start=True, stop=True).then_inc(ranks_done, 1)
                ob = r * NQB

                def invert(s, b, first, last_):
                    pe.wait_ge(oh_ready, s + (ob + 1))
                    for q in range(QB):
                        last = nc.tensor.matmul(ps_l[:, 0:2 * ET], ohb[b][:, q, :], oha[b][:, q, :, :].rearrange("p a t -> p (a t)"),
                                                start=(first and q == 0), stop=(last_ and q == QB - 1))
                    last.then_inc(inv_used, 1)
                    return last

                invert(0, 0, True, False)
                invert(1, 1, False, False)
                with pe.Fori(0, NQB // 2 - 2) as j:
                    invert(j * 2 + 2, 0, False, False)
                    invert(j * 2 + 3, 1, False, False)
                invert(NQB - 2, 0, False, False)
                pe.wait_ge(oh_ready, ob + NQB)
                for q in range(QB):
                    last = nc.tensor.matmul(ps_l[:, 0:2 * ET], ohb[1][:, q, :], oha[1][:, q, :, :].rearrange("p a t -> p (a t)"),
                                            start=False, stop=(q == QB - 1))
                last.then_inc(inv_done, 1)

            def experts(r):
                base = r * ET

                def rows_in(t, h, p, first):
                    pe.wait_ge(xg_in[p], (h + (r * PAR[p] + 1)) * 16)
                    if not first:
                        pe.wait_ge(xt_ready, t + base)
                    for c in range(DC):
                        last = nc.tensor.transpose(ps_x[:, c * P:(c + 1) * P], xg[p][:, c * P:(c + 1) * P], ident[:])
                    last.then_inc(xg_tr, 1)

                def up(p, w_sb, dst, e, done):
                    for c in range(DC):
                        last = nc.tensor.matmul(dst[p][:], xt[p][:, c, :], w_sb[:, bass.ds(e * DC + c, 1), :].rearrange("p a i -> p (a i)"),
                                                start=(c == 0), stop=(c == DC - 1))
                    last.then_inc(done, 1)

                def hidden_in(t, p, first):
                    pe.wait_ge(f_ready, t + (base + 1))
                    if not first:
                        pe.wait_ge(ft_ready, t + base)
                    for c in range(IC):
                        last = nc.tensor.transpose(ps_f[:, c * P:(c + 1) * P], fu[p][:, c * P:(c + 1) * P], ident[:])
                    last.then_inc(f_tr, 1)

                def down(t, p, e, first):
                    pe.wait_ge(ft_ready, t + (base + 1))
                    if not first:
                        pe.wait_ge(ye_ready, t + base)
                    for c in range(IC):
                        last = nc.tensor.matmul(ps_u[:, 0:D], ft[p][:, c, :], w2_sb[:, bass.ds(e * IC + c, 1), :].rearrange("p a d -> p (a d)"),
                                                start=(c == 0), stop=(c == IC - 1))
                    last.then_inc(ye_done, 1)

                def expert_of(t):
                    return pe.value_load(eid[0:1, bass.ds(t, 1)], min_val=0, max_val=E - 1)

                def tile(t, h, p, first, last):
                    e = expert_of(t)
                    pe.wait_ge(xt_ready, t + (base + 1))
                    if not (isinstance(t, int) and t < 2):
                        pe.wait_ge(f_ready, t + (base - 1))
                    up(p, w11_sb, ps_g, e, g_done)
                    if not first:
                        hidden_in(t - 1, 1 - p, isinstance(t, int) and t == 1)
                    up(p, w12_sb, ps_v, e, v_done)
                    if not first:
                        down(t - 1, 1 - p, expert_of(t - 1), isinstance(t, int) and t == 1)
                    if not last:
                        rows_in(t + 1, h + p, 1 - p, False)

                pe.wait_ge(slots_ready, r + 1)
                pe.wait_ge(s_expw, 48)
                rows_in(0, 0, 0, True)
                tile(0, 0, 0, True, False)
                tile(1, 0, 1, False, False)
                tile(2, 1, 0, False, False)
                with pe.Fori(0, (ET - 5) // 2) as h:
                    tile(h * 2 + 3, h + 1, 1, False, False)
                    tile(h * 2 + 4, h + 2, 0, False, False)
                tile(ET - 2, (ET - 2) // 2, 1, False, False)
                tile(ET - 1, (ET - 1) // 2, 0, False, True)
                hidden_in(ET - 1, 0, False)
                down(ET - 1, 0, expert_of(ET - 1), False)

            route_chunk(0, 0, 0, True)
            route_chunk(1, 1, 1, False)
            with pe.Fori(0, NCH // 2 - 1) as j:
                for b in range(2):
                    route_chunk(j * 2 + (b + 2), j * 2 + (b + 2), b, False)
            router(0)
            experts(0)

            pe.wait_ge(s_attw, 32)

            def mixer_in(i, b):
                pe.wait_ge(tn_ready, i + 1)
                pe.wait_ge(xnt_ready, i + NCH)
                transposes(b)
                pe.wait_ge(xnt_ready, i + (NCH + 1))
                for jc in range(2 * DC):
                    if not (isinstance(i, int) and i == 0):
                        pe.wait_ge(xz_ready, i * 4 + (jc - 3))
                    for c in range(DC):
                        last = nc.tensor.matmul(ps_p[jc][:], inw_sb[:, c, jc * P:(jc + 1) * P], xnt[b][:, c, :], start=(c == 0), stop=(c == DC - 1))
                    last.then_inc(proj_done, 1)

            def ssm_in(c, first):
                pe.wait_ge(conv_ready, c + 1)
                if not first:
                    pe.wait_ge(u_ready, c)
                for h in range(DC):
                    last = nc.tensor.matmul(ps_u[:], wct_sb[:, h, :], mix[:, h, :], start=(h == 0), stop=(h == DC - 1))
                last.then_inc(u_done, 1)

            mixer_in(0, 0)
            mixer_in(1, 1)
            ssm_in(0, True)
            with pe.Fori(0, NCH // 2 - 1) as j:
                mixer_in(j * 2 + 2, 0)
                ssm_in(j * 2 + 1, False)
                mixer_in(j * 2 + 3, 1)
                ssm_in(j * 2 + 2, False)
            ssm_in(NCH - 1, False)

            with pe.Fori(0, NCH // 2) as j:
                for b in range(2):
                    i = j * 2 + b
                    pe.wait_ge(bwd_done, i + 2)
                    for h in range(DC):
                        last = nc.tensor.matmul(ps_p[h][:], woc_sb[:, h * P:(h + 1) * P], states[:, b, :], start=True, stop=True)
                    last.then_inc(y_done, 1)
                    pe.wait_ge(yg_ready, i + 1)
                    for t in range(G):
                        for h in range(DC):
                            last = nc.tensor.matmul(ps_p[2 + t // 2][:, (t % 2) * D:(t % 2 + 1) * D], mix[:, h, t * P:(t + 1) * P], outw_sb[:, h, :],
                                                    start=(h == 0), stop=(h == DC - 1))
                    last.then_inc(o_done, 1)
                    route_chunk(i + 2 * NCH, i + NCH, b, False)
            router(1)
            experts(1)


def kernel(**inputs):
    import numpy as np
    import concourse.bacc as bacc
    from concourse.bass_utils import run_bass_kernel_spmd

    a = {k[3:]: np.ascontiguousarray(v) for k, v in inputs.items()}
    f = {k[5:]: v for k, v in a.items() if k.startswith("attn_")}
    per_part = lambda v: v.reshape(-1, P).T
    both = lambda k: np.concatenate([f["f_" + k], f["b_" + k]]).reshape(P, 1)
    step = np.concatenate([np.broadcast_to(f["f_logdt"].reshape(1), (N,)), np.broadcast_to(f["b_logdt"].reshape(1), (N,))]).reshape(P, 1)
    cols = np.concatenate([per_part(f["norm_scale"]), per_part(f["in_b"]),
                           f["dw_w"].reshape(DC, P, 3).transpose(1, 0, 2).reshape(P, 6), per_part(f["dw_b"]), per_part(f["pw_b"]),
                           both("logA"), both("B"), both("C"), step], axis=1)
    arrays = {
        "x": f["T"].reshape(L, D), "wg": a["ffn_Wg"], "w11": a["ffn_W11"], "w12": a["ffn_W12"], "w2": a["ffn_W2"],
        "in_wt": f["in_w"].T, "pw": f["pw_w"], "wint": np.concatenate([f["f_win"], f["b_win"]], axis=0).T,
        "woutt": np.concatenate([f["f_wout"], f["b_wout"]], axis=1).T, "out_wt": f["out_w"].T,
        "out_b": f["out_b"].reshape(1, D), "cols": cols,
    }
    arrays = {k: np.ascontiguousarray(v) for k, v in arrays.items()}
    nc = bacc.Bacc("TRN2", target_bir_lowering=False, num_devices=1)
    ins = [nc.dram_tensor(k, v.shape, mybir.dt.from_np(v.dtype), kind="ExternalInput").ap() for k, v in arrays.items()]
    out = nc.dram_tensor("out_rows", [ROWS, D], F32, kind="ExternalOutput").ap()
    build(nc, *ins, out)
    r = run_bass_kernel_spmd(nc, [arrays], core_ids=[0])
    return r.results[0]["out_rows"][0:L].reshape(1, L, D)
```

```python
from contextlib import ExitStack

import concourse.bass as bass
from concourse import mybir

F32 = mybir.dt.float32
I32 = mybir.dt.int32
U32 = mybir.dt.uint32
ALU = mybir.AluOpType
ACT = mybir.ActivationFunctionType
AX = mybir.AxisListType

P = 128
L, D = 4096, 256
E, I, TOPK = 8, 512, 2
N = 64
DC, IC = D // P, I // P
NT = L // P
G = 4
CH = G * P
NCH = NT // G
ET = L * TOPK // P + E - 1
NQ = NT * TOPK
QB = 4
NQB = NQ // QB
ROWS = L + P
LN_EPS, RMS_EPS, SUM_EPS, A_EPS = 1e-5, 1e-6, 1e-8, 1e-6

C_NS, C_INB, C_DWW, C_DWB, C_PWB, C_LOGA, C_B, C_C, C_LOGDT = 0, 2, 6, 12, 14, 16, 17, 18, 19
NCOLS = 20


def build(nc, x, wg, w11, w12, w2, in_wt, pw, wint, woutt, out_wt, out_b, cols, out):
    ctx = ExitStack()
    with ctx:
        def sb(name, shape, dt=F32):
            return ctx.enter_context(nc.sbuf_tensor(name, shape, dt))

        def sem(name):
            return ctx.enter_context(nc.semaphore(name))

        xn_dram = nc.dram_tensor("xn_rows", [ROWS, D], F32, kind="Internal").ap()
        x1_dram = nc.dram_tensor("x1_rows", [ROWS, D], F32, kind="Internal").ap()

        w11_sb = sb("w11_sb", [P, E * DC, I])
        w12_sb = sb("w12_sb", [P, E * DC, I])
        w2_sb = sb("w2_sb", [P, E * IC, D])
        wg_sb = sb("wg_sb", [P, DC, E])
        inw_sb = sb("inw_sb", [P, DC, 2 * D])
        outw_sb = sb("outw_sb", [P, DC, D])
        wct_sb = sb("wct_sb", [P, DC, P])
        woc_sb = sb("woc_sb", [P, D])
        outb_sb = sb("outb_sb", [P, D])
        col = sb("col", [P, NCOLS])

        ident = sb("ident", [P, P])
        iota_row = sb("iota_row", [P, P])
        e_rank = sb("e_rank", [P, E])
        tok_id = sb("tok_id", [P, NT, TOPK])
        ln_eps = sb("ln_eps", [P, G])
        neg_half = sb("neg_half", [P, 2, G])
        pad_id = sb("pad_id", [P, 1])
        ssm = sb("ssm", [P, 12])
        a_mask = sb("a_mask", [P, 1], U32)
        ABAR, BBAR, UB, EXPA, DT, AA, ADT, DEN, RDEN, FRAC, ONE = range(11)

        seq = sb("seq", [P, DC, L + 3])
        gate = sb("gate", [P, DC, L])
        states = sb("states", [P, 2, CH])
        work = sb("work", [P, 7168])
        logits = sb("logits", [P, NT, E])
        idx_i = sb("idx_i", [P, ET], I32)
        w_slot = sb("w_slot", [P, ET])
        eid = sb("eid", [P, ET], I32)
        idx_g = [sb(f"idx_g{p}", [P, 1], I32) for p in range(2)]
        idx_s = sb("idx_s", [P, 1], I32)
        bnst = sb("bnst", [P, 2, G, 6])
        mv = sb("mv", [P, 2, G, 2])
        vars_ = sb("vars_", [P, 2, 2, G])
        rstd = sb("rstd", [P, 2, 2, G])
        x1_mean = sb("x1_mean", [P, NT])
        x1_rstd = sb("x1_rstd", [P, NT])
        fence = sb("fence", [P, 1])

        def part(at, *shape):
            n = 1
            for s in shape:
                n *= s
            v = work[:, at:at + n]
            if len(shape) == 2:
                v = v.rearrange("p (a b) -> p a b", b=shape[1])
            if len(shape) == 3:
                v = v.rearrange("p (a b c) -> p a b c", b=shape[1], c=shape[2])
            return v

        xin = [part(b * 1024, G, D) for b in range(2)]
        xn = [part(2048 + b * 1024, G, D) for b in range(2)]
        xnt = [part(4096 + b * 1024, DC, CH) for b in range(2)]
        mix = part(6144, DC, CH)
        R = [part(k * 256, NT * E) for k in range(10)]
        tok = [part(2560 + k * 64, NT, TOPK) for k in range(8)]
        small = part(3072, 256)
        ohb = [part(3328 + b * 512, QB, P) for b in range(2)]
        oha = [part(4352 + b * 568, QB, 2, ET) for b in range(2)]
        eqa = [part(5504 + b * 284, QB, ET) for b in range(2)]
        before = part(6144, P)
        ones = part(6272, P)
        seg = part(6400, E, NT)
        xg = [part(b * 256, D) for b in range(2)]
        xt = [part(512 + b * 256, DC, P) for b in range(2)]
        sg = [part(1024 + b * 512, I) for b in range(2)]
        fu = [part(2048 + b * 512, I) for b in range(2)]
        ft = [part(3072 + b * 512, IC, P) for b in range(2)]
        yb = [part(4096 + b * 256, D) for b in range(2)]
        pw_sb = part(6144, DC, D)
        wint_sb = part(6656, DC, P)
        woutt_sb = part(6912, D)
        zeros = states[:, 0, 0:D]
        iota_i = sb("iota_i", [P, P], I32)

        bank = [ctx.enter_context(nc.psum_tensor(f"bank{k}", [P, 512], F32)) for k in range(8)]
        ps_t = bank[0:2]
        ps_p = bank[2:6]
        ps_l = bank[6]
        ps_u = bank[7]
        ps_x, ps_f = bank[0], bank[1]
        ps_g, ps_v = bank[2:4], bank[4:6]

        s_cols, s_setw, s_wg, s_attw, s_expw = (sem(n) for n in ("s_cols", "s_setw", "s_wg", "s_attw", "s_expw"))
        inw_ready = sem("inw_ready")
        pool_const, const_ready = sem("pool_const"), sem("const_ready")
        ssm_exp, ssm_step, ssm_ready, wct_done, wct_ready = (sem(n) for n in ("ssm_exp", "ssm_step", "ssm_ready", "wct_done", "wct_ready"))
        pads_out = sem("pads_out")
        x1_out = [sem(f"x1_out{b}") for b in range(2)]
        x_in = [sem(f"x_in{b}") for b in range(2)]
        x_out = [sem(f"x_out{b}") for b in range(2)]
        xn_out = [sem(f"xn_out{b}") for b in range(2)]
        ln_step, mv_ready, rstd_step, rstd_ready, norm_ready = (sem(n) for n in ("ln_step", "mv_ready", "rstd_step", "rstd_ready", "norm_ready"))
        tr_done, xnt_ready, logits_done, logits_copied = (sem(n) for n in ("tr_done", "xnt_ready", "logits_done", "logits_copied"))
        kept, t_ready, res_step, res_ready = (sem(n) for n in ("kept", "t_ready", "res_step", "res_ready"))
        proj_done, xz_ready, states_in = sem("proj_done"), sem("xz_ready"), sem("states_in")
        conv_step, conv_ready, u_done, u_ready, fwd_done = (sem(n) for n in ("conv_step", "conv_ready", "u_done", "u_ready", "fwd_done"))
        bwd_done, y_done, yg_ready, o_done, x2_ready = (sem(n) for n in ("bwd_done", "y_done", "yg_ready", "o_done", "x2_ready"))
        route_step, route_exp, ranks_done, route_const, oh_ready, id_ready, score_ready, inv_used, inv_done, slots_ready = (
            sem(n) for n in ("route_step", "route_exp", "ranks_done", "route_const", "oh_ready", "id_ready", "score_ready", "inv_used", "inv_done", "slots_ready"))
        gather_idx, scatter_idx = sem("gather_idx"), sem("scatter_idx")
        xg_in = [sem(f"xg_in{p}") for p in range(2)]
        xg_tr, xt_ready, g_done, v_done, sg_ready, f_step, f_ready = (sem(n) for n in ("xg_tr", "xt_ready", "g_done", "v_done", "sg_ready", "f_step", "f_ready"))
        f_tr, ft_ready, ye_done, ye_ready, added = (sem(n) for n in ("f_tr", "ft_ready", "ye_done", "ye_ready", "added"))

        block = ctx.enter_context(nc.Block())

        def rows(dram, c):
            return dram[bass.ds(c * CH, CH), :].rearrange("(j p) d -> p j d", p=P)

        RS = 40
        PAR = [(ET + 1) // 2, ET // 2]

        @block.sync
        def _(sp):
            for b in range(2):
                sp.dma_start(xin[b], rows(x, b)).then_inc(x_in[b], 16)
            sp.dma_start(wg_sb[:], wg.rearrange("(c p) e -> p c e", p=P)).then_inc(s_wg, 16)
            sp.dma_start(pw_sb, pw.rearrange("(c p) d -> p c d", p=P)).then_inc(s_setw, 16)
            sp.dma_start(wint_sb, wint.rearrange("(c p) n -> p c n", p=P)).then_inc(s_setw, 16)
            sp.dma_start(woutt_sb, woutt).then_inc(s_setw, 16)

            def store_rows(j, b):
                c = j * 2 + b
                sp.wait_ge(x_in[b], j * 16 + 16)
                sp.dma_start(rows(x1_dram, c), xin[b]).then_inc(x1_out[b], 16)
                sp.wait_ge(norm_ready, c + 1)
                sp.dma_start(rows(xn_dram, c), xn[b]).then_inc(xn_out[b], 16)

            with sp.Fori(0, NCH // 2 - 1) as j:
                for b in range(2):
                    store_rows(j, b)
                    sp.wait_ge(x1_out[b], j * 16 + 16)
                    sp.dma_start(xin[b], rows(x, j * 2 + b + 2)).then_inc(x_in[b], 16)
            for b in range(2):
                store_rows(NCH // 2 - 1, b)
            sp.wait_ge(const_ready, 1)
            for dram in (xn_dram, x1_dram, out):
                sp.dma_start(dram[L:ROWS, :], zeros).then_inc(pads_out, 16)
            sp.dma_start(w11_sb[:], w11.rearrange("e (c p) i -> p (e c) i", p=P)).then_inc(s_expw, 16)
            sp.dma_start(w12_sb[:], w12.rearrange("e (c p) i -> p (e c) i", p=P)).then_inc(s_expw, 16)
            sp.dma_start(w2_sb[:], w2.rearrange("e (c p) d -> p (e c) d", p=P)).then_inc(s_expw, 16)
            sp.dma_start(inw_sb[:], in_wt.rearrange("(c p) n -> p c n", p=P)).then_inc(s_attw, 16)
            sp.dma_start(outw_sb[:], out_wt.rearrange("(c p) n -> p c n", p=P)).then_inc(s_attw, 16)
            sp.dma_start(outb_sb[:], out_b.to_broadcast([P, D])).then_inc(s_attw, 16)

            sp.wait_ge(added, 16 * ET)
            for b in range(2):
                sp.dma_start(xin[b], rows(x1_dram, b)).then_inc(x_in[b], 16)
            with sp.Fori(0, NCH // 2 - 1) as j:
                for b in range(2):
                    sp.wait_ge(norm_ready, j * 2 + (NCH + b + 1))
                    sp.dma_start(xin[b], rows(x1_dram, j * 2 + b + 2)).then_inc(x_in[b], 16)

            for b in range(2):
                sp.wait_ge(norm_ready, 2 * NCH - 1 + b)
                sp.dma_start(xin[b], rows(x1_dram, NCH - 1 - b)).then_inc(x_in[b], 16)

            def store_x2(i, b, c):
                sp.wait_ge(x2_ready, i + 1)
                sp.dma_start(rows(out, c), xin[b]).then_inc(x_out[b], 16)
                sp.wait_ge(norm_ready, i + (2 * NCH + 1))
                sp.dma_start(rows(xn_dram, c), xn[b]).then_inc(xn_out[b], 16)

            with sp.Fori(0, NCH // 2 - 1) as j:
                for b in range(2):
                    ahead = j * -2 + (NCH - 3 - b)
                    store_x2(j * 2 + b, b, j * -2 + (NCH - 1 - b))
                    sp.wait_ge(x_out[b], j * 16 + 16)
                    sp.dma_start(xin[b], rows(x1_dram, ahead)).then_inc(x_in[b], 16)
            for b in range(2):
                store_x2(NCH - 2 + b, b, 1 - b)
            sp.wait_ge(pads_out, 48)
            for b in range(2):
                sp.wait_ge(x1_out[b], 16 * (NCH // 2))
                sp.wait_ge(x_out[b], 16 * (NCH // 2))
                sp.wait_ge(xn_out[b], 16 * NCH)
            sp.wait_ge(added, 2 * 16 * ET)

        @block.gpsimd
        def _(pool):
            step = 0
            def link(ins):
                nonlocal step
                step += 1
                ins.then_inc(pool_const, 1)
                pool.wait_ge(pool_const, step)

            nc.gpsimd.memset(zeros, 0.0)
            nc.gpsimd.memset(neg_half[:], -0.5)
            nc.gpsimd.memset(ln_eps[:], LN_EPS)
            nc.gpsimd.memset(ssm[:, ONE:ONE + 1], 1.0)
            link(nc.gpsimd.memset(ident[:], 0.0))
            nc.gpsimd.affine_select(out=ident[:], in_=ident[:], compare_op=ALU.not_equal, fill=1.0, base=0,
                                    pattern=[[-1, P]], channel_multiplier=1)
            link(nc.gpsimd.iota(iota_i[:], pattern=[[1, P]], base=0, channel_multiplier=0))
            link(nc.gpsimd.tensor_copy(iota_row[:], iota_i[:]))
            link(nc.gpsimd.iota(iota_i[:, 0:E], pattern=[[-1, E]], base=E, channel_multiplier=0))
            link(nc.gpsimd.tensor_copy(e_rank[:], iota_i[:, 0:E]))
            link(nc.gpsimd.iota(iota_i[:, 0:1], pattern=[[1, 1]], base=L + 1, channel_multiplier=1))
            link(nc.gpsimd.tensor_copy(pad_id[:], iota_i[:, 0:1]))
            link(nc.gpsimd.iota(iota_i[:, 0:NQ], pattern=[[P, NT], [0, TOPK]], base=1, channel_multiplier=1))
            nc.gpsimd.tensor_copy(tok_id[:].rearrange("p t k -> p (t k)"), iota_i[:, 0:NQ]).then_inc(const_ready, 1)

            def rsqrt_ln(k, b):
                pool.wait_ge(mv_ready, k + 1)
                nc.gpsimd.tensor_tensor(vars_[:, b, 0, :], mv[:, b, :, 1], ln_eps[:], ALU.add).then_inc(rstd_step, 1)
                pool.wait_ge(rstd_step, k + 1)
                nc.gpsimd.tensor_tensor(rstd[:, b, 0, :], vars_[:, b, 0, :], neg_half[:, 0, :], ALU.pow).then_inc(rstd_ready, 1)

            def rsqrt_rms(i, b):
                k = i + NCH
                pool.wait_ge(mv_ready, k + 1)
                nc.gpsimd.tensor_copy(x1_mean[:, bass.ds(i * G, G)], mv[:, b, :, 0])
                nc.gpsimd.tensor_scalar(vars_[:, b, 1, :], mv[:, b, :, 1], 1.0 + RMS_EPS, LN_EPS * RMS_EPS, ALU.mult, ALU.add)
                nc.gpsimd.tensor_tensor(vars_[:, b, 0, :], mv[:, b, :, 1], ln_eps[:], ALU.add).then_inc(rstd_step, 1)
                pool.wait_ge(rstd_step, k + 1)
                nc.gpsimd.tensor_tensor(rstd[:, b, :, :], vars_[:, b, :, :], neg_half[:], ALU.pow).then_inc(rstd_ready, 1)
                pool.wait_ge(rstd_ready, k + 1)
                nc.gpsimd.tensor_copy(x1_rstd[:, bass.ds(i * G, G)], rstd[:, b, 0, :]).then_inc(kept, 1)

            def residual(i, b):
                pool.wait_ge(t_ready, i + 1)
                nc.gpsimd.tensor_tensor(xin[b], xin[b], xn[b], ALU.add).then_inc(res_step, 1)
                pool.wait_ge(res_step, i + 1)
                nc.gpsimd.tensor_tensor(xin[b], xin[b], outb_sb[:].unsqueeze(1).to_broadcast([P, G, D]), ALU.add).then_inc(res_ready, 1)

            def route_consts(r):
                if r == 0:
                    pool.wait_ge(wct_ready, 1)
                else:
                    pool.wait_ge(o_done, NCH)
                nc.gpsimd.memset(before, 1.0)
                nc.gpsimd.memset(ones, 1.0)
                link(nc.gpsimd.memset(seg, 1.0))
                nc.gpsimd.affine_select(out=before, in_=before, compare_op=ALU.is_gt, fill=0.0, base=0,
                                        pattern=[[1, P]], channel_multiplier=-1)
                nc.gpsimd.memset(seg[:, :, 0], 0.0).then_inc(route_const, 1)

            def id_onehots(r):
                with pool.Fori(0, NQB // 2) as j:
                    for b in range(2):
                        s = j * 2 + b
                        pool.wait_ge(oh_ready, s + (r * NQB + 1))
                        ids = tok_id[:].rearrange("p t k -> p (t k)")[:, bass.ds(s * QB, QB)].unsqueeze(2)
                        nc.gpsimd.tensor_tensor(oha[b][:, :, 0, :], eqa[b], ids.to_broadcast([P, QB, ET]), ALU.mult).then_inc(id_ready, 1)

            def experts(r):
                base = r * ET

                def gather(t, p):
                    done = t + (base - 1)
                    pool.wait_ge(xg_tr, done)
                    nc.gpsimd.tensor_copy(idx_g[p][:], idx_i[:, bass.ds(t, 1)]).then_inc(gather_idx, 1)
                    pool.wait_ge(pads_out, 48)
                    pool.wait_ge(gather_idx, done)
                    nc.gpsimd.indirect_dma_start(xg[p], None, xn_dram, bass.IndirectOffsetOnAxis(ap=idx_g[p][:], axis=0)).then_inc(xg_in[p], 16)

                def scatter(t, p, first=False):
                    done = t + (base + 1)
                    pool.wait_ge(ye_ready, done)
                    if not (first and r == 0):
                        pool.wait_ge(added, t * 16 + 16 * base)
                    nc.gpsimd.tensor_copy(idx_s[:], idx_i[:, bass.ds(t, 1)]).then_inc(scatter_idx, 1)
                    dst = x1_dram if r == 0 else out
                    pool.wait_ge(pads_out, 48)
                    pool.wait_ge(scatter_idx, done)
                    nc.gpsimd.indirect_dma_start(dst, bass.IndirectOffsetOnAxis(ap=idx_s[:], axis=0), yb[p], None,
                                                 compute_op=ALU.add).then_inc(added, 16)

                pool.wait_ge(slots_ready, r + 1)
                for b in range(2):
                    pool.wait_ge(xn_out[b], 16 * (NCH // 2) * (r + 1))
                pool.wait_ge(pads_out, 48)
                for b in range(2):
                    pool.wait_ge([x1_out, x_out][r][b], 16 * (NCH // 2))
                for t in range(2):
                    copy = nc.gpsimd.tensor_copy(idx_g[t][:], idx_i[:, t:t + 1])
                    if r == 0:
                        link(copy)
                    else:
                        copy.then_inc(gather_idx, 1)
                        pool.wait_ge(gather_idx, base - 1 + t)
                    nc.gpsimd.indirect_dma_start(xg[t], None, xn_dram, bass.IndirectOffsetOnAxis(ap=idx_g[t][:], axis=0)).then_inc(xg_in[t], 16)
                gather(2, 0)
                gather(3, 1)
                scatter(0, 0, first=True)
                with pool.Fori(0, (ET - 5) // 2) as h:
                    for p in range(2):
                        gather(h * 2 + (4 + p), p)
                        scatter(h * 2 + (1 + p), 1 - p)
                gather(ET - 1, (ET - 1) % 2)
                for t in range(ET - 4, ET):
                    scatter(t, t % 2)

            with pool.Fori(0, NCH // 2) as j:
                for b in range(2):
                    rsqrt_ln(j * 2 + b, b)
            route_consts(0)
            id_onehots(0)
            experts(0)
            with pool.Fori(0, NCH // 2) as j:
                for b in range(2):
                    rsqrt_rms(j * 2 + b, b)
            pool.wait_ge(s_attw, 48)
            with pool.Fori(0, NCH // 2) as j:
                for b in range(2):
                    residual(j * 2 + b, b)
                    rsqrt_ln(j * 2 + (b + 2 * NCH), b)
            route_consts(1)
            id_onehots(1)
            experts(1)

        @block.scalar
        def _(act):
            act.dma_start(col[:], cols).then_inc(s_cols, 16)
            act.wait_ge(s_cols, 16)
            nc.scalar.activation(ssm[:, EXPA:EXPA + 1], col[:, C_LOGA:C_LOGA + 1], ACT.Exp).then_inc(ssm_exp, 1)
            nc.scalar.activation(ssm[:, DT:DT + 1], col[:, C_LOGDT:C_LOGDT + 1], ACT.Exp).then_inc(ssm_exp, 1)
            act.wait_ge(ssm_step, 2)
            nc.scalar.activation(ssm[:, ABAR:ABAR + 1], ssm[:, ADT:ADT + 1], ACT.Exp).then_inc(ssm_exp, 1)

            def rows_t(k, b):
                act.wait_ge(tr_done, k + 1)
                for h in range(DC):
                    last = nc.scalar.activation(xnt[b][:, h, :], ps_t[h][:], ACT.Copy)
                last.then_inc(xnt_ready, 1)

            def logits_out(n, c):
                act.wait_ge(logits_done, n + 1)
                nc.scalar.activation(logits[:, bass.ds(c * G, G), :].rearrange("p t e -> p (t e)"), ps_l[:, 0:G * E], ACT.Copy).then_inc(logits_copied, 1)

            def router_exp(r):
                act.wait_ge(route_step, r * RS + 2)
                nc.scalar.activation(R[1], R[0], ACT.Exp).then_inc(route_exp, 1)
                scores = tok[1].rearrange("p t k -> p (t k)")
                with act.Fori(0, NQB // 2) as j:
                    for b in range(2):
                        s = j * 2 + b
                        act.wait_ge(oh_ready, s + (r * NQB + 1))
                        for q in range(QB):
                            last = nc.scalar.activation(oha[b][:, q, 1, :], eqa[b][:, q, :], ACT.Copy, scale=scores[:, bass.ds(s * QB + q, 1)])
                        last.then_inc(score_ready, 1)

            def experts(r):
                base = r * ET

                def finish(t, p, first_ring):
                    act.wait_ge(f_tr, t + (base + 1))
                    act.wait_ge(ye_done, t + (base - 1)) if not first_ring else None
                    nc.scalar.activation(ft[p].rearrange("p c k -> p (c k)"), ps_f[:], ACT.Copy).then_inc(ft_ready, 1)
                    act.wait_ge(ye_done, t + (base + 1))
                    act.wait_ge(added, t * 16 + 16 * (base - 1)) if not first_ring else None
                    nc.scalar.activation(yb[p], ps_u[:, 0:D], ACT.Copy, scale=w_slot[:, bass.ds(t, 1)]).then_inc(ye_ready, 1)

                def tile(t, h, p, first, last):
                    act.wait_ge(g_done, t + (base + 1))
                    if not first:
                        act.wait_ge(f_step, t + (base - 1)) if not (isinstance(t, int) and t < 2) else None
                    nc.scalar.activation(sg[p], ps_g[p][:], ACT.Sigmoid).then_inc(sg_ready, 1)
                    if not first:
                        finish(t - 1, 1 - p, False)

                act.wait_ge(slots_ready, r + 1)
                tile(0, 0, 0, True, False)
                act.wait_ge(g_done, base + 2)
                nc.scalar.activation(sg[1], ps_g[1][:], ACT.Sigmoid).then_inc(sg_ready, 1)
                finish(0, 0, True)
                act.wait_ge(g_done, base + 3)
                act.wait_ge(f_step, base + 1)
                nc.scalar.activation(sg[0], ps_g[0][:], ACT.Sigmoid).then_inc(sg_ready, 1)
                finish(1, 1, True)
                with act.Fori(0, (ET - 3) // 2) as h:
                    tile(h * 2 + 3, h, 1, False, False)
                    tile(h * 2 + 4, h, 0, False, False)
                finish(ET - 1, 0, False)

            rows_t(0, 0)
            rows_t(1, 1)
            logits_out(0, 0)
            with act.Fori(0, NCH // 2 - 1) as j:
                for b in range(2):
                    k = j * 2 + (b + 2)
                    rows_t(k, b)
                    logits_out(j * 2 + (b + 1), j * 2 + (b + 1))
            logits_out(NCH - 1, NCH - 1)
            router_exp(0)
            experts(0)

            def project(i, last):
                i2, b = i
                for jc in range(2 * DC):
                    if jc == DC and not last:
                        rows_t(i2 + (NCH + 1), 1 - b)
                    act.wait_ge(proj_done, i2 * (2 * DC) + (jc + 1))
                    if jc < DC:
                        nc.scalar.activation(seq[:, jc, bass.ds(i2 * CH + 2, CH)], ps_p[jc][:], ACT.Identity,
                                             bias=col[:, C_INB + jc:C_INB + jc + 1]).then_inc(xz_ready, 1)
                    else:
                        nc.scalar.activation(gate[:, jc - DC, bass.ds(i2 * CH, CH)], ps_p[jc][:], ACT.Sigmoid,
                                             bias=col[:, C_INB + jc:C_INB + jc + 1]).then_inc(xz_ready, 1)

            rows_t(NCH, 0)
            with act.Fori(0, NCH // 2 - 1) as j:
                for b in range(2):
                    project((j * 2 + b, b), False)
            project((NCH - 2, 0), False)
            project((NCH - 1, 1), True)

            def take_states(i, b, c):
                nc.scalar.activation(states[:, b, :], seq[:, 0, bass.ds(c * CH + 1, CH)], ACT.Copy).then_inc(states_in, 1)

            act.wait_ge(fwd_done, NCH + 1)
            act.wait_ge(bwd_done, 1)
            take_states(0, 0, NCH - 1)
            act.wait_ge(bwd_done, 2)
            take_states(1, 1, NCH - 2)
            with act.Fori(0, NCH // 2 - 1) as j:
                for b in range(2):
                    i = j * 2 + b
                    act.wait_ge(y_done, i + 1)
                    act.wait_ge(bwd_done, i + 3)
                    take_states(i + 2, b, j * -2 + (NCH - 3 - b))
                    rows_t(i + 2 * NCH, b)
                    logits_out(i + NCH, j * -2 + (NCH - 1 - b))
            for b in range(2):
                rows_t(3 * NCH - 2 + b, b)
                logits_out(2 * NCH - 2 + b, 1 - b)
            router_exp(1)
            experts(1)

        @block.vector
        def _(dve):
            def chain(sem_, start):
                at = [start]

                def link(ins, wait=True):
                    at[0] += 1
                    ins.then_inc(sem_, 1)
                    if wait:
                        dve.wait_ge(sem_, at[0])
                return link, at

            link, at = chain(ssm_step, 0)
            v = lambda k: ssm[:, k:k + 1]
            dve.wait_ge(const_ready, 1)
            dve.wait_ge(ssm_exp, 2)
            link(nc.vector.tensor_scalar(v(AA), v(EXPA), -1.0, None, ALU.mult))
            link(nc.vector.tensor_tensor(v(ADT), v(AA), v(DT), ALU.mult))
            nc.vector.tensor_scalar(a_mask[:], v(EXPA), A_EPS, None, ALU.is_lt)
            link(nc.vector.tensor_copy(v(DEN), v(AA)))
            link(nc.vector.copy_predicated(v(DEN), a_mask[:], v(ONE)))
            link(nc.vector.reciprocal(v(RDEN), v(DEN)))
            dve.wait_ge(ssm_exp, 3)
            link(nc.vector.tensor_scalar(v(FRAC), v(ABAR), -1.0, v(RDEN), ALU.add, ALU.mult))
            link(nc.vector.copy_predicated(v(FRAC), a_mask[:], v(DT)))
            link(nc.vector.tensor_tensor(v(BBAR), v(FRAC), col[:, C_B:C_B + 1], ALU.mult))
            def ln_stats(k, b):
                for t in range(G):
                    last = nc.vector.bn_stats(bnst[:, b, t, :], xin[b][:, t, :])
                last.then_inc(ln_step, 1)
                dve.wait_ge(ln_step, k + 1)
                nc.vector.memset(fence[:], 0.0)
                for t in range(G):
                    last = nc.vector.bn_aggr(mv[:, b, t, :], bnst[:, b, t, :])
                last.then_inc(mv_ready, 1)

            def ln_apply(k, b, which):
                dve.wait_ge(rstd_ready, k + 1)
                for t in range(G):
                    last = nc.vector.tensor_scalar(xn[b][:, t, :], xin[b][:, t, :], mv[:, b, t, 0:1], rstd[:, b, which, t:t + 1], ALU.subtract, ALU.mult)
                last.then_inc(norm_ready, 1)

            def router(r):
                link, at = chain(route_step, r * RS)
                grid = lambda a: a.rearrange("p (t e) -> p t e", e=E)
                cols_ = lambda a: a.rearrange("p (e t) -> p e t", e=E)
                flip = lambda a: a.rearrange("p (e t) -> p t e", e=E)
                over_e = lambda a: a.unsqueeze(2).to_broadcast([P, NT, E])
                rank = e_rank[:].unsqueeze(1).to_broadcast([P, NT, E])
                lg = logits[:]
                s0, s1, s2, s3 = (small[:, k * NT:(k + 1) * NT] for k in range(4))
                best = [tok[0][:, :, k] for k in range(TOPK)]
                dve.wait_ge(route_const, r + 1)
                dve.wait_ge(logits_copied, NCH * (r + 1))
                for b in range(2):
                    dve.wait_ge(xn_out[b], 16 * (NCH // 2) * (r + 1))
                    dve.wait_ge([x1_out, x_out][r][b], 16 * (NCH // 2))
                link(nc.vector.reduce_max(s0, lg, AX.X))
                link(nc.vector.tensor_tensor(grid(R[0]), lg, over_e(s0), ALU.subtract))
                dve.wait_ge(route_exp, r + 1)
                link(nc.vector.reduce_sum(s1, grid(R[1]), AX.X))
                link(nc.vector.reciprocal(s2, s1))
                link(nc.vector.tensor_tensor(grid(R[2]), grid(R[1]), over_e(s2), ALU.mult))
                onehot = [R[5], R[8]]
                prob = R[2]
                for k in range(TOPK):
                    link(nc.vector.reduce_max(best[k], grid(prob), AX.X))
                    link(nc.vector.tensor_tensor(grid(R[3]), grid(prob), over_e(best[k]), ALU.is_equal))
                    link(nc.vector.tensor_tensor(grid(R[4]), grid(R[3]), rank, ALU.mult))
                    link(nc.vector.reduce_max(s3, grid(R[4]), AX.X))
                    link(nc.vector.tensor_tensor(flip(onehot[k]), over_e(s3), rank, ALU.is_equal))
                    if k == 0:
                        link(nc.vector.scalar_tensor_tensor(grid(R[6]), flip(onehot[0]), -2.0, grid(prob), ALU.mult, ALU.add))
                        prob = R[6]
                link(nc.vector.tensor_tensor(R[9], onehot[0], onehot[1], ALU.add))
                link(nc.vector.tensor_tensor(s0, best[0], best[1], ALU.add))
                link(nc.vector.tensor_scalar(s1, s0, SUM_EPS, None, ALU.add))
                link(nc.vector.reciprocal(s2, s1))
                for k in range(TOPK):
                    last = nc.vector.scalar_tensor_tensor(tok[1][:, :, k], best[k], 0.5, s2, ALU.mult, ALU.mult)
                link(last)
                cnt, tiles_i, tiles, ends, first = (small[:, 128 + 8 * k:136 + 8 * k] for k in range(5))
                dve.wait_ge(ranks_done, r + 1)
                rank_ps, tot_ps = ps_u[:, 0:NT * E], ps_u[:, NT * E:2 * NT * E]
                link(nc.vector.tensor_copy(R[0], tot_ps))
                nc.vector.reduce_sum(cnt, cols_(R[0]), AX.X)
                link(nc.vector.tensor_tensor_scan(R[1], seg.rearrange("p e t -> p (e t)"), R[0], 0.0, ALU.mult, ALU.add))
                link(nc.vector.tensor_scalar(tiles_i.bitcast(I32), cnt, float(P - 1), None, ALU.add))
                link(nc.vector.tensor_scalar(tiles_i.bitcast(I32), tiles_i.bitcast(I32), 7, None, ALU.logical_shift_right))
                link(nc.vector.tensor_copy(tiles, tiles_i.bitcast(I32)))
                link(nc.vector.tensor_tensor_scan(ends, ones[:, 0:E], tiles, 0.0, ALU.mult, ALU.add))
                link(nc.vector.tensor_tensor(first, ends, tiles, ALU.subtract))
                link(nc.vector.tensor_tensor(R[1], R[1], R[0], ALU.subtract))
                link(nc.vector.tensor_tensor(R[2], rank_ps, R[1], ALU.add))
                link(nc.vector.scalar_tensor_tensor(cols_(R[3]), first.unsqueeze(2).to_broadcast([P, E, NT]), float(P), cols_(R[2]), ALU.mult, ALU.add))
                for k in range(TOPK):
                    last = nc.vector.tensor_tensor([R[4], R[7]][k], onehot[k], R[3], ALU.mult)
                link(last)
                for k in range(TOPK):
                    last = nc.vector.reduce_sum(tok[2][:, :, k], flip([R[4], R[7]][k]), AX.X)
                link(last)
                ge = R[0][:, 0:(E - 1) * 32]
                flat = lambda a: a.rearrange("p t k -> p (t k)")
                link(nc.vector.tensor_copy(flat(tok[3]).bitcast(I32), flat(tok[2])))
                nc.vector.tensor_scalar(flat(tok[4]).bitcast(I32), flat(tok[3]).bitcast(I32), P - 1, None, ALU.bitwise_and)
                link(nc.vector.tensor_scalar(flat(tok[5]).bitcast(I32), flat(tok[3]).bitcast(I32), 7, None, ALU.logical_shift_right))
                nc.vector.tensor_copy(flat(tok[6]), flat(tok[4]).bitcast(I32))
                link(nc.vector.tensor_copy(flat(tok[7]), flat(tok[5]).bitcast(I32)))
                big = work[:, 0:ET * (E - 1)].rearrange("p (t e) -> p t e", e=E - 1)
                link(nc.vector.tensor_tensor(big, iota_row[:, 0:ET].unsqueeze(2).to_broadcast([P, ET, E - 1]),
                                             ends[:, 0:E - 1].unsqueeze(1).to_broadcast([P, ET, E - 1]), ALU.is_ge))
                link(nc.vector.reduce_sum(R[2][:, 0:ET], big, AX.X))
                link(nc.vector.tensor_copy(eid[:], R[2][:, 0:ET]))
                ob = r * NQB

                def onehots(s, b, free):
                    if free:
                        dve.wait_ge(inv_used, s + (ob - 1))
                    q = bass.ds(s * QB, QB)
                    place, tile_ = (flat(a)[:, q].unsqueeze(2) for a in (tok[6], tok[7]))
                    nc.vector.tensor_tensor(ohb[b], iota_row[:].unsqueeze(1).to_broadcast([P, QB, P]), place.to_broadcast([P, QB, P]), ALU.is_equal)
                    nc.vector.tensor_tensor(eqa[b], iota_row[:, 0:ET].unsqueeze(1).to_broadcast([P, QB, ET]), tile_.to_broadcast([P, QB, ET]), ALU.is_equal).then_inc(oh_ready, 1)

                onehots(0, 0, False)
                onehots(1, 1, False)
                with dve.Fori(0, NQB // 2 - 1) as j:
                    onehots(j * 2 + 2, 0, True)
                    onehots(j * 2 + 3, 1, True)
                dve.wait_ge(inv_done, r + 1)
                inv_id, inv_w = ps_l[:, 0:ET], ps_l[:, ET:2 * ET]
                nc.vector.tensor_copy(w_slot[:], inv_w)
                link(nc.vector.tensor_scalar(R[2][:, 0:ET], inv_id, 0.0, pad_id[:], ALU.is_equal, ALU.mult))
                nc.vector.scalar_tensor_tensor(idx_i[:], inv_id, -1.0, R[2][:, 0:ET], ALU.add, ALU.add).then_inc(slots_ready, 1)
                dve.wait_ge(slots_ready, r + 1)
                assert at[0] == (r + 1) * RS, at[0] - r * RS

            def experts(r):
                base = r * ET

                def rows_in(t, p):
                    dve.wait_ge(xg_tr, t + (base + 1))
                    nc.vector.tensor_copy(xt[p].rearrange("p c k -> p (c k)"), ps_x[:, 0:D]).then_inc(xt_ready, 1)

                def tile(t, p, last):
                    dve.wait_ge(sg_ready, t + (base + 1))
                    nc.vector.tensor_tensor(sg[p], sg[p], ps_g[p][:], ALU.mult).then_inc(f_step, 1)
                    if not last:
                        rows_in(t + 1, 1 - p)
                    dve.wait_ge(f_step, t + (base + 1))
                    dve.wait_ge(v_done, t + (base + 1))
                    nc.vector.tensor_tensor(fu[p], sg[p], ps_v[p][:], ALU.mult).then_inc(f_ready, 1)

                rows_in(0, 0)
                with dve.Fori(0, ET // 2) as h:
                    tile(h * 2, 0, False)
                    tile(h * 2 + 1, 1, False)
                tile(ET - 1, 0, True)

            def norm_x(k, j, b):
                dve.wait_ge(tr_done, k - 1)
                dve.wait_ge(xn_out[b], j * 16)
                ln_apply(k, b, 0)

            for b in range(2):
                dve.wait_ge(x_in[b], 16)
                ln_stats(b, b)
            ln_apply(0, 0, 0)
            dve.wait_ge(x_in[0], 32)
            ln_stats(2, 0)
            ln_apply(1, 1, 0)
            with dve.Fori(0, NCH // 2 - 2) as j:
                for b in range(2):
                    dve.wait_ge(x_in[1 - b], j * 16 + 16 * (2 + b))
                    ln_stats(j * 2 + (b + 3), 1 - b)
                    norm_x(j * 2 + (b + 2), j + 1, b)
            dve.wait_ge(x_in[1], 16 * (NCH // 2))
            ln_stats(NCH - 1, 1)
            for b in range(2):
                norm_x(NCH - 2 + b, NCH // 2 - 1, b)

            dve.wait_ge(s_setw, 48)
            dve.wait_ge(s_cols, 16)
            nc.vector.tensor_scalar(woc_sb[:], woutt_sb, col[:, C_C:C_C + 1], None, ALU.mult)
            dve.wait_ge(wct_done, 1)
            nc.vector.tensor_copy(wct_sb[:].rearrange("p c n -> p (c n)"), ps_p[0][:, 0:D])
            nc.vector.tensor_copy(v(UB), ps_p[1][:, 0:1]).then_inc(wct_ready, 1)
            dve.wait_ge(wct_ready, 1)
            router(0)
            experts(0)

            def stats_x1(i, m, b):
                dve.wait_ge(x_in[b], m * 16 + 16 * (NCH // 2 + 1))
                ln_stats(i + NCH, b)

            def norm_x1(i, b):
                dve.wait_ge(tr_done, i + (NCH - 1))
                ln_apply(i + NCH, b, 1)

            def convolve(c):
                dww = lambda h, k: col[:, C_DWW + 3 * h + k:C_DWW + 3 * h + k + 1]
                last_c = isinstance(c, int) and c == NCH - 1
                dve.wait_ge(xz_ready, NCH * 4 if last_c else c * 4 + (4 + DC))
                if not (isinstance(c, int) and c == 0):
                    dve.wait_ge(u_done, c)
                for h in range(DC):
                    last = nc.vector.tensor_scalar(mix[:, h, :], seq[:, h, bass.ds(c * CH + 2, CH)], dww(h, 1), col[:, C_DWB + h:C_DWB + h + 1], ALU.mult, ALU.add)
                last.then_inc(conv_step, 1)
                dve.wait_ge(conv_step, c * 2 + 1)
                for h in range(DC):
                    last = nc.vector.scalar_tensor_tensor(mix[:, h, :], seq[:, h, bass.ds(c * CH + 1, CH)], dww(h, 0), mix[:, h, :], ALU.mult, ALU.add)
                last.then_inc(conv_step, 1)
                dve.wait_ge(conv_step, c * 2 + 2)
                for h in range(DC):
                    last = nc.vector.scalar_tensor_tensor(mix[:, h, :], seq[:, h, bass.ds(c * CH + 3, CH)], dww(h, 2), mix[:, h, :], ALU.mult, ALU.add)
                last.then_inc(conv_ready, 1)

            def scan_forward(c):
                here = seq[:, 0, bass.ds(c * CH + 1, CH)]
                dve.wait_ge(conv_ready, c + 1)
                dve.wait_ge(u_done, c + 1)
                nc.vector.tensor_scalar(here, ps_u[:], v(UB), v(BBAR), ALU.add, ALU.mult).then_inc(u_ready, 1)
                dve.wait_ge(u_ready, c + 2)
                dve.wait_ge(fwd_done, c + 1)
                nc.vector.tensor_tensor_scan(here[0:N], ssm[0:N, ABAR:ABAR + 1].to_broadcast([N, CH]), here[0:N],
                                             seq[0:N, 0, bass.ds(c * CH, 1)], ALU.mult, ALU.add).then_inc(fwd_done, 1)

            nc.vector.memset(seq[:, :, 0:2], 0.0).then_inc(u_ready, 1)
            nc.vector.memset(seq[:, :, L + 2:L + 3], 0.0).then_inc(fwd_done, 1)
            dve.wait_ge(s_attw, 48)
            for c in range(DC):
                last = nc.vector.tensor_scalar(inw_sb[:, c, :], inw_sb[:, c, :], col[:, C_NS + c:C_NS + c + 1], None, ALU.mult)
            last.then_inc(inw_ready, 1)
            for b in range(2):
                stats_x1(b, 0, b)
            for b in range(2):
                norm_x1(b, b)
            stats_x1(2, 1, 0)
            norm_x1(2, 0)
            stats_x1(3, 1, 1)
            convolve(0)
            norm_x1(3, 1)
            with dve.Fori(0, NCH // 2 - 2) as j:
                for b in range(2):
                    i = j * 2 + (b + 4)
                    scan_forward(j * 2 + b)
                    stats_x1(i, j + 2, b)
                    convolve(j * 2 + (b + 1))
                    norm_x1(i, b)
            for c in range(NCH - 3, NCH):
                scan_forward(c - 1)
                convolve(c)
            scan_forward(NCH - 1)

            def scan_backward(i, b):
                dve.wait_ge(states_in, i + 1)
                dve.wait_ge(bwd_done, i + 1)
                back = states[N:P, b, ::-1]
                nc.vector.tensor_tensor_scan(back, ssm[N:P, ABAR:ABAR + 1].to_broadcast([N, CH]), back,
                                             states[N:P, 1 - b, 0:1], ALU.mult, ALU.add).then_inc(bwd_done, 1)

            def norm_t(i, m, b, c):
                dve.wait_ge(kept, NCH)
                dve.wait_ge(tr_done, i + (2 * NCH - 1))
                dve.wait_ge(xn_out[b], m * 16 + 16 * (NCH // 2))
                dve.wait_ge(x_in[b], m * 16 + 16 * (NCH + 1))
                for t in range(G):
                    last = nc.vector.tensor_scalar(xn[b][:, t, :], xin[b][:, t, :], x1_mean[:, bass.ds(c * G + t, 1)], x1_rstd[:, bass.ds(c * G + t, 1)],
                                                   ALU.subtract, ALU.mult)
                last.then_inc(t_ready, 1)

            def gate_y(i, c):
                dve.wait_ge(y_done, i + 1)
                for h in range(DC):
                    last = nc.vector.tensor_tensor(mix[:, h, :], gate[:, h, bass.ds(c * CH, CH)], ps_p[h][:], ALU.mult)
                last.then_inc(yg_ready, 1)

            def add_mixer(i, b):
                dve.wait_ge(res_ready, i + 1)
                dve.wait_ge(o_done, i + 1)
                for h in range(2):
                    last = nc.vector.tensor_tensor(xin[b][:, 2 * h:2 * h + 2, :].rearrange("p t d -> p (t d)"),
                                                   xin[b][:, 2 * h:2 * h + 2, :].rearrange("p t d -> p (t d)"), ps_p[2 + h][:], ALU.add)
                last.then_inc(x2_ready, 1)
                dve.wait_ge(x2_ready, i + 1)
                ln_stats(i + 2 * NCH, b)

            nc.vector.memset(states[N:P, 1, 0:1], 0.0).then_inc(bwd_done, 1)
            norm_t(0, 0, 0, NCH - 1)
            scan_backward(0, 0)
            gate_y(0, NCH - 1)
            scan_backward(1, 1)
            with dve.Fori(0, NCH // 2 - 1) as j:
                for b in range(2):
                    i, c = j * 2 + b, j * -2 + (NCH - 2 - b)
                    add_mixer(i, b)
                    norm_t(i + 1, j + b, 1 - b, c)
                    gate_y(i + 1, c)
                    ln_apply(i + 2 * NCH, b, 0)
                    scan_backward(i + 2, b)
            add_mixer(NCH - 2, 0)
            norm_t(NCH - 1, NCH // 2 - 1, 1, 0)
            gate_y(NCH - 1, 0)
            ln_apply(3 * NCH - 2, 0, 0)
            add_mixer(NCH - 1, 1)
            ln_apply(3 * NCH - 1, 1, 0)
            router(1)
            experts(1)

        @block.tensor
        def _(pe):
            def transposes(k, b):
                pe.wait_ge(norm_ready, k + 1)
                if not (isinstance(k, int) and k == 0):
                    pe.wait_ge(xnt_ready, k)
                for t in range(G):
                    for h in range(DC):
                        last = nc.tensor.transpose(ps_t[h][:, t * P:(t + 1) * P], xn[b][:, t, h * P:(h + 1) * P], ident[:])
                last.then_inc(tr_done, 1)

            def route_chunk(k, n, b):
                pe.wait_ge(xnt_ready, k + 1)
                if not (isinstance(n, int) and n == 0):
                    pe.wait_ge(logits_copied, n)
                for t in range(G):
                    for h in range(DC):
                        last = nc.tensor.matmul(ps_l[:, t * E:(t + 1) * E], xnt[b][:, h, t * P:(t + 1) * P], wg_sb[:, h, :],
                                                start=(h == 0), stop=(h == DC - 1))
                last.then_inc(logits_done, 1)

            def fold():
                pe.wait_ge(s_setw, 48)
                pe.wait_ge(s_cols, 16)
                for dc in range(DC):
                    for ec in range(DC):
                        nc.tensor.matmul(ps_p[0][:, dc * P:(dc + 1) * P], pw_sb[:, ec, dc * P:(dc + 1) * P], wint_sb[:, ec, :],
                                         start=(ec == 0), stop=(ec == DC - 1))
                for ec in range(DC):
                    last = nc.tensor.matmul(ps_p[1][:, 0:1], wint_sb[:, ec, :], col[:, C_PWB + ec:C_PWB + ec + 1], start=(ec == 0), stop=(ec == DC - 1))
                last.then_inc(wct_done, 1)

            def router(r):
                pe.wait_ge(route_step, r * RS + 17)
                nc.tensor.matmul(ps_u[:, 0:NT * E], before, R[9], start=True, stop=True)
                nc.tensor.matmul(ps_u[:, NT * E:2 * NT * E], ones, R[9], start=True, stop=True).then_inc(ranks_done, 1)
                ob = r * NQB

                def invert(s, b, first=False, done=inv_used):
                    pe.wait_ge(id_ready, s + (ob + 1))
                    pe.wait_ge(score_ready, s + (ob + 1))
                    for q in range(QB):
                        last = nc.tensor.matmul(ps_l[:, 0:2 * ET], ohb[b][:, q, :], oha[b][:, q, :, :].rearrange("p a t -> p (a t)"),
                                                start=(first and q == 0), stop=(done is inv_done and q == QB - 1))
                    last.then_inc(done, 1)

                invert(0, 0, first=True)
                invert(1, 1)
                with pe.Fori(0, NQB // 2 - 2) as j:
                    invert(j * 2 + 2, 0)
                    invert(j * 2 + 3, 1)
                invert(NQB - 2, 0)
                invert(NQB - 1, 1, done=inv_done)

            def experts(r):
                base = r * ET

                def rows_in(t, h, p, first):
                    pe.wait_ge(xg_in[p], (h + (r * PAR[p] + 1)) * 16)
                    if not first:
                        pe.wait_ge(xt_ready, t + base)
                    for c in range(DC):
                        last = nc.tensor.transpose(ps_x[:, c * P:(c + 1) * P], xg[p][:, c * P:(c + 1) * P], ident[:])
                    last.then_inc(xg_tr, 1)

                def up(p, w_sb, dst, e, done):
                    for c in range(DC):
                        last = nc.tensor.matmul(dst[p][:], xt[p][:, c, :], w_sb[:, bass.ds(e * DC + c, 1), :].rearrange("p a i -> p (a i)"),
                                                start=(c == 0), stop=(c == DC - 1))
                    last.then_inc(done, 1)

                def hidden_in(t, p, first):
                    pe.wait_ge(f_ready, t + (base + 1))
                    if not first:
                        pe.wait_ge(ft_ready, t + base)
                    for c in range(IC):
                        last = nc.tensor.transpose(ps_f[:, c * P:(c + 1) * P], fu[p][:, c * P:(c + 1) * P], ident[:])
                    last.then_inc(f_tr, 1)

                def down(t, p, e, first):
                    pe.wait_ge(ft_ready, t + (base + 1))
                    if not first:
                        pe.wait_ge(ye_ready, t + base)
                    for c in range(IC):
                        last = nc.tensor.matmul(ps_u[:, 0:D], ft[p][:, c, :], w2_sb[:, bass.ds(e * IC + c, 1), :].rearrange("p a d -> p (a d)"),
                                                start=(c == 0), stop=(c == IC - 1))
                    last.then_inc(ye_done, 1)

                def expert_of(t):
                    return pe.value_load(eid[0:1, bass.ds(t, 1)], min_val=0, max_val=E - 1)

                def tile(t, h, p, first=False, last=False):
                    e = expert_of(t)
                    pe.wait_ge(xt_ready, t + (base + 1))
                    if not (isinstance(t, int) and t < 2):
                        pe.wait_ge(f_ready, t + (base - 1))
                    up(p, w11_sb, ps_g, e, g_done)
                    if not first:
                        hidden_in(t - 1, 1 - p, isinstance(t, int) and t == 1)
                    if not last:
                        rows_in(t + 1, h + p, 1 - p, False)
                    up(p, w12_sb, ps_v, e, v_done)
                    if not first:
                        down(t - 1, 1 - p, expert_of(t - 1), isinstance(t, int) and t == 1)

                pe.wait_ge(slots_ready, r + 1)
                pe.wait_ge(s_expw, 48)
                rows_in(0, 0, 0, True)
                tile(0, 0, 0, first=True)
                tile(1, 0, 1)
                tile(2, 1, 0)
                with pe.Fori(0, (ET - 5) // 2) as h:
                    tile(h * 2 + 3, h + 1, 1)
                    tile(h * 2 + 4, h + 2, 0)
                tile(ET - 2, (ET - 2) // 2, 1)
                tile(ET - 1, (ET - 1) // 2, 0, last=True)
                hidden_in(ET - 1, 0, False)
                down(ET - 1, 0, expert_of(ET - 1), False)

            pe.wait_ge(const_ready, 1)
            transposes(0, 0)
            transposes(1, 1)
            pe.wait_ge(s_wg, 16)
            route_chunk(0, 0, 0)
            fold()
            with pe.Fori(0, NCH // 2 - 1) as j:
                for b in range(2):
                    k = j * 2 + (b + 1)
                    transposes(k + 1, b)
                    route_chunk(k, k, 1 - b)
            route_chunk(NCH - 1, NCH - 1, 1)
            router(0)
            experts(0)

            def project(i, b, last=False):
                first = isinstance(i, int) and i == 0
                for jc in range(2 * DC):
                    if jc == 0:
                        pe.wait_ge(xnt_ready, i + (NCH + 1))
                    if jc == DC and not last:
                        transposes(i + (NCH + 1), 1 - b)
                    if not first:
                        pe.wait_ge(xz_ready, i * 4 + (jc - 3))
                    for c in range(DC):
                        mm = nc.tensor.matmul(ps_p[jc][:], inw_sb[:, c, jc * P:(jc + 1) * P], xnt[b][:, c, :], start=(c == 0), stop=(c == DC - 1))
                    mm.then_inc(proj_done, 1)

            def ssm_in(c):
                pe.wait_ge(conv_ready, c + 1)
                pe.wait_ge(u_ready, c + 1)
                for h in range(DC):
                    last = nc.tensor.matmul(ps_u[:], wct_sb[:, h, :], mix[:, h, :], start=(h == 0), stop=(h == DC - 1))
                last.then_inc(u_done, 1)

            pe.wait_ge(s_attw, 48)
            transposes(NCH, 0)
            pe.wait_ge(inw_ready, 1)
            project(0, 0)
            with pe.Fori(0, NCH // 2 - 1) as j:
                for b in range(2):
                    project(j * 2 + (b + 1), 1 - b)
                    ssm_in(j * 2 + b)
            project(NCH - 1, 1, last=True)
            ssm_in(NCH - 2)
            ssm_in(NCH - 1)

            def ssm_out(i, b):
                pe.wait_ge(bwd_done, i + 2)
                if not (isinstance(i, int) and i == 0):
                    pe.wait_ge(yg_ready, i)
                for h in range(DC):
                    last = nc.tensor.matmul(ps_p[h][:], woc_sb[:, h * P:(h + 1) * P], states[:, b, :], start=True, stop=True)
                last.then_inc(y_done, 1)

            def project_out(i):
                pe.wait_ge(yg_ready, i + 1)
                if not (isinstance(i, int) and i == 0):
                    pe.wait_ge(x2_ready, i)
                for t in range(G):
                    for h in range(DC):
                        last = nc.tensor.matmul(ps_p[2 + t // 2][:, (t % 2) * D:(t % 2 + 1) * D], mix[:, h, t * P:(t + 1) * P], outw_sb[:, h, :],
                                                start=(h == 0), stop=(h == DC - 1))
                last.then_inc(o_done, 1)

            ssm_out(0, 0)
            project_out(0)
            ssm_out(1, 1)
            with pe.Fori(0, NCH // 2 - 1) as j:
                for b in range(2):
                    i = j * 2 + (b + 1)
                    project_out(i)
                    transposes(j * 2 + (b + 2 * NCH), b)
                    ssm_out(i + 1, b)
                    route_chunk(j * 2 + (b + 2 * NCH), j * 2 + (b + NCH), b)
            project_out(NCH - 1)
            transposes(3 * NCH - 2, 0)
            route_chunk(3 * NCH - 2, 2 * NCH - 2, 0)
            transposes(3 * NCH - 1, 1)
            route_chunk(3 * NCH - 1, 2 * NCH - 1, 1)
            router(1)
            experts(1)


def kernel(**inputs):
    import numpy as np
    import concourse.bacc as bacc
    from concourse.bass_utils import run_bass_kernel_spmd

    a = {k[3:]: np.ascontiguousarray(v) for k, v in inputs.items()}
    f = {k[5:]: v for k, v in a.items() if k.startswith("attn_")}
    per_part = lambda v: v.reshape(-1, P).T
    both = lambda k: np.concatenate([f["f_" + k], f["b_" + k]]).reshape(P, 1)
    step = np.concatenate([np.broadcast_to(f["f_logdt"].reshape(1), (N,)), np.broadcast_to(f["b_logdt"].reshape(1), (N,))]).reshape(P, 1)
    cols = np.concatenate([per_part(f["norm_scale"]), per_part(f["in_b"]),
                           f["dw_w"].reshape(DC, P, 3).transpose(1, 0, 2).reshape(P, 6), per_part(f["dw_b"]), per_part(f["pw_b"]),
                           both("logA"), both("B"), both("C"), step], axis=1)
    arrays = {
        "x": f["T"].reshape(L, D), "wg": a["ffn_Wg"], "w11": a["ffn_W11"], "w12": a["ffn_W12"], "w2": a["ffn_W2"],
        "in_wt": f["in_w"].T, "pw": f["pw_w"], "wint": np.concatenate([f["f_win"], f["b_win"]], axis=0).T,
        "woutt": np.concatenate([f["f_wout"], f["b_wout"]], axis=1).T, "out_wt": f["out_w"].T,
        "out_b": f["out_b"].reshape(1, D), "cols": cols,
    }
    arrays = {k: np.ascontiguousarray(v) for k, v in arrays.items()}
    nc = bacc.Bacc("TRN2", target_bir_lowering=False, num_devices=1)
    ins = [nc.dram_tensor(k, v.shape, mybir.dt.from_np(v.dtype), kind="ExternalInput").ap() for k, v in arrays.items()]
    out = nc.dram_tensor("out_rows", [ROWS, D], F32, kind="ExternalOutput").ap()
    build(nc, *ins, out)
    r = run_bass_kernel_spmd(nc, [arrays], core_ids=[0])
    return r.results[0]["out_rows"][0:L].reshape(1, L, D)
```

```python
from contextlib import ExitStack

import concourse.bass as bass
from concourse import mybir

F32 = mybir.dt.float32
F32R = mybir.dt.float32r
I32 = mybir.dt.int32
U32 = mybir.dt.uint32
ALU = mybir.AluOpType
ACT = mybir.ActivationFunctionType
AX = mybir.AxisListType

P = 128
L, D = 4096, 256
E, I, TOPK = 8, 512, 2
N = 64
DC, IC = D // P, I // P
NT = L // P
G = 4
CH = G * P
NCH = NT // G
ET = L * TOPK // P + E - 1
NQ = NT * TOPK
QB = 4
NQB = NQ // QB
ROWS = L + P
LN_EPS, RMS_EPS, SUM_EPS, A_EPS = 1e-5, 1e-6, 1e-8, 1e-6

C_NS, C_INB, C_DWW, C_DWB, C_PWB, C_LOGA, C_B, C_C, C_LOGDT = 0, 2, 6, 12, 14, 16, 17, 18, 19
NCOLS = 20


def build(nc, x, wg, w11, w12, w2, in_wt, pw, wint, woutt, out_wt, out_b, cols, out):
    ctx = ExitStack()
    with ctx:
        def sb(name, shape, dt=F32):
            return ctx.enter_context(nc.sbuf_tensor(name, shape, dt))

        def sem(name):
            return ctx.enter_context(nc.semaphore(name))

        xn_dram = nc.dram_tensor("xn_rows", [ROWS, D], F32, kind="Internal").ap()
        x1_dram = nc.dram_tensor("x1_rows", [ROWS, D], F32, kind="Internal").ap()
        w11_lo_dram = nc.dram_tensor("w11_lo_rows", [P, E * DC * I], F32, kind="Internal").ap()
        w12_lo_dram = nc.dram_tensor("w12_lo_rows", [P, E * DC * I], F32, kind="Internal").ap()
        w2_lo_dram = nc.dram_tensor("w2_lo_rows", [P, E * IC * D], F32, kind="Internal").ap()

        w11_hi = sb("w11_hi", [P, E * DC, I], F32R)
        w12_hi = sb("w12_hi", [P, E * DC, I], F32R)
        with nc.sbuf_tensor("x_all", [P, NT, D], F32) as x_all:
            pass
        w2_raw = x_all[:]
        w2_hi = sb("w2_hi", [P, E * IC, D], F32R)
        wg_sb = sb("wg_sb", [P, DC, E])
        inw_sb = sb("inw_sb", [P, DC, 2 * D])
        outw_sb = sb("outw_sb", [P, DC, D])
        wct_sb = sb("wct_sb", [P, DC, P])
        woc_sb = sb("woc_sb", [P, D])
        outb_sb = sb("outb_sb", [P, D])
        col = sb("col", [P, NCOLS])

        ident = sb("ident", [P, P])
        iota_row = sb("iota_row", [P, P])
        e_rank = sb("e_rank", [P, E])
        tok_id = sb("tok_id", [P, NT, TOPK])
        ln_eps = sb("ln_eps", [P, G])
        neg_half = sb("neg_half", [P, G])
        pad_id = sb("pad_id", [P, 1])
        ssm = sb("ssm", [P, 12])
        a_mask = sb("a_mask", [P, 1], U32)
        ABAR, BBAR, UB, EXPA, DT, AA, ADT, DEN, RDEN, FRAC, ONE = range(11)

        with nc.sbuf_tensor("seq", [P, DC, L + 8], F32) as seq, nc.sbuf_tensor("gate", [P, DC, L], F32) as gate:
            pass
        w11_lo = sb("w11_lo", [P, E * DC * I + DC * 8], F32R)[:, 0:E * DC * I].rearrange("p (k i) -> p k i", i=I)
        w12_lo = sb("w12_lo", [P, E * DC, I], F32R)[:]
        w11_raw = seq[:].rearrange("p h l -> p (h l)")[:, 0:E * DC * I].rearrange("p (k i) -> p k i", i=I)
        w12_raw = gate[:].rearrange("p h l -> p (h l)").rearrange("p (k i) -> p k i", i=I)
        with nc.sbuf_tensor("states", [P, 2, CH], F32) as states:
            pass
        xt_hi = [sb(f"xt_hi{b}", [P, DC, P], F32R)[:] for b in range(2)]
        xt_lo = [sb(f"xt_lo{b}", [P, DC, P], F32R)[:] for b in range(2)]
        with nc.sbuf_tensor("work", [P, 7168], F32) as work:
            pass
        xg = [sb(f"xg{b}", [P, D])[:] for b in range(2)]
        ft_lo = [sb(f"ft_lo{b}", [P, IC, P], F32R)[:] for b in range(2)]
        sg = [sb(f"sg{b}", [P, I])[:] for b in range(2)]
        fu = [sb(f"fu{b}", [P, I])[:] for b in range(2)]
        ft_hi = [sb(f"ft_hi{b}", [P, IC, P], F32R)[:] for b in range(2)]
        yb = [sb(f"yb{b}", [P, D])[:] for b in range(2)]
        w2_lo = sb("w2_lo", [P, 2 * IC, D], F32R)[:]
        logits = sb("logits", [P, NT, E])
        idx_i = sb("idx_i", [P, ET], I32)
        w_slot = sb("w_slot", [P, ET])
        eid = sb("eid", [P, ET + 2], I32)
        tile_ends = sb("tile_ends", [P, E], I32)
        idx_g = [sb(f"idx_g{p}", [P, 1], I32) for p in range(2)]
        idx_s = sb("idx_s", [P, 1], I32)
        bnst = sb("bnst", [P, 2, G, 6])
        mv = sb("mv", [P, 2, G, 2])
        vars_ = sb("vars_", [P, 2, 2, G])
        rstd = sb("rstd", [P, 2, 2, G])
        x1_mean = sb("x1_mean", [P, NT])
        x1_rstd = sb("x1_rstd", [P, NT])
        fence, table = sb("fence", [P, 1]), sb("table", [P, 1])

        def part(at, *shape):
            n = 1
            for s in shape:
                n *= s
            v = work[:, at:at + n]
            if len(shape) == 2:
                v = v.rearrange("p (a b) -> p a b", b=shape[1])
            if len(shape) == 3:
                v = v.rearrange("p (a b c) -> p a b c", b=shape[1], c=shape[2])
            return v

        xin = [part(b * 1024, G, D) for b in range(2)]
        xn = [part(2048 + b * 1024, G, D) for b in range(2)]
        xnt = [part(4096 + b * 1024, DC, CH) for b in range(2)]
        mix = part(6144, DC, CH)
        conv = [mix, states[:]]
        t_rows, x2 = ([seq[:, 1, at + b * 1024:at + (b + 1) * 1024].rearrange("p (t d) -> p t d", d=D) for b in range(2)] for at in (0, 2048))
        R = [part(k * 256, NT * E) for k in range(10)]
        tok = [part(2560 + k * 64, NT, TOPK) for k in range(8)]
        small = part(3072, 256)
        ohb = [part(at, QB, P) for at in (3328, 3840, 0, 1364)]
        oha = [part(at, QB, 2, ET) for at in (4352, 4920, 512, 1876)]
        eqa = [part(at, QB, ET) for at in (5504, 5788, 1080, 6656)]
        before = part(6144, P)
        ones = part(6272, P)
        seg = part(6400, E, NT)
        past_end, past_ends = part(6072, ET, E - 1), part(6072 + ET * (E - 1), ET)
        pw_sb = part(6144, DC, D)
        wint_sb = part(6656, DC, P)
        woutt_sb = part(6912, D)
        zeros = states[:, 0, 0:D]
        w2_piece = [a[:, h, :] for a in (inw_sb, states) for h in range(2)]
        iota_i = sb("iota_i", [P, P], I32)

        bank = [ctx.enter_context(nc.psum_tensor(f"bank{k}", [P, 512], F32)) for k in range(8)]
        ps_t = bank[0:2]
        ps_p = bank[2:6]
        ps_l = bank[6]
        ps_u = bank[7]
        ps_x, ps_f = bank[0], bank[1]
        ps_g, ps_v = bank[2:4], bank[4:6]

        s_cols, s_setw, s_wg, s_attw = (sem(n) for n in ("s_cols", "s_setw", "s_wg", "s_attw"))
        s_w2 = [sem(f"s_w2_{b}") for b in range(4)]
        w2_hi_ready, w2_lo_pool, w2_lo_dve, w2_lo_in = sem("w2_hi_ready"), sem("w2_lo_pool"), sem("w2_lo_dve"), sem("w2_lo_in")
        w2_lo_out = [sem(f"w2_lo_out{b}") for b in range(4)]
        inw_ready = sem("inw_ready")
        pool_const, const_ready = sem("pool_const"), sem("const_ready")
        ssm_exp, ssm_step, ssm_ready, wct_done, wct_ready = (sem(n) for n in ("ssm_exp", "ssm_step", "ssm_ready", "wct_done", "wct_ready"))
        pads_out = sem("pads_out")
        w11_in = [sem(f"w11_in{b}") for b in range(2)]
        w12_in = [sem(f"w12_in{b}") for b in range(2)]
        hi11_ready, hi12_ready, lo11_ready, lo12_ready, lo_out, lo_in, xt_step = (sem(n) for n in ("hi11_ready", "hi12_ready", "lo11_ready", "lo12_ready", "lo_out", "lo_in", "xt_step"))
        x1_out = sem("x1_out")
        x_in = [sem(f"x_in{b}") for b in range(2)]
        x_out = [sem(f"x_out{b}") for b in range(2)]
        xn_out = [sem(f"xn_out{b}") for b in range(2)]
        ln_step, mv_ready, rstd_step, rstd_ready, norm_ready = (sem(n) for n in ("ln_step", "mv_ready", "rstd_step", "rstd_ready", "norm_ready"))
        tr_done, xnt_ready, logits_done, logits_copied = (sem(n) for n in ("tr_done", "xnt_ready", "logits_done", "logits_copied"))
        neg_mean, t_step = sem("neg_mean"), sem("t_step")
        kept, t_ready, res_step, res_ready = (sem(n) for n in ("kept", "t_ready", "res_step", "res_ready"))
        proj_done, xz_ready, states_in = sem("proj_done"), sem("xz_ready"), sem("states_in")
        conv_step, conv_ready, u_done, u_ready, fwd_done = (sem(n) for n in ("conv_step", "conv_ready", "u_done", "u_ready", "fwd_done"))
        bwd_done, y_done, yg_ready, o_done, x2_ready = (sem(n) for n in ("bwd_done", "y_done", "yg_ready", "o_done", "x2_ready"))
        route_step, route_exp, ranks_done, route_const, oh_ready, id_ready, score_ready, inv_used, inv_done, slots_ready = (
            sem(n) for n in ("route_step", "route_exp", "ranks_done", "route_const", "oh_ready", "id_ready", "score_ready", "inv_used", "inv_done", "slots_ready"))
        gather_idx, scatter_idx = sem("gather_idx"), sem("scatter_idx")
        xg_in = [sem(f"xg_in{p}") for p in range(2)]
        xg_tr, xt_ready, g_done, v_done, sg_ready, f_step, f_ready = (sem(n) for n in ("xg_tr", "xt_ready", "g_done", "v_done", "sg_ready", "f_step", "f_ready"))
        f_tr, ft_hi_ready, ft_ready, ye_done, ye_ready, added = (sem(n) for n in ("f_tr", "ft_hi_ready", "ft_ready", "ye_done", "ye_ready", "added"))

        block = ctx.enter_context(nc.Block())

        def rows(dram, c):
            return dram[bass.ds(c * CH, CH), :].rearrange("(j p) d -> p j d", p=P)

        RS = 40
        PAR = [(ET + 1) // 2, ET // 2]
        W2_PIECES = E * IC // 2
        W2_POOL = W2_PIECES - 4

        @block.sync
        def _(sp):
            def load_x(c, b):
                sp.dma_start(x_all[:, bass.ds(c * G, G), :], rows(x, c)).then_inc(x_in[b], 16)

            for b in range(2):
                load_x(b, b)
            sp.dma_start(wg_sb[:], wg.rearrange("(c p) e -> p c e", p=P)).then_inc(s_wg, 16)
            with sp.Fori(0, NCH // 2 - 1) as j:
                for b in range(2):
                    sp.wait_ge(x_in[b], j * 16 + 16)
                    load_x(j * 2 + (b + 2), b)
            sp.dma_start(pw_sb, pw.rearrange("(c p) d -> p c d", p=P)).then_inc(s_setw, 16)
            sp.dma_start(wint_sb, wint.rearrange("(c p) n -> p c n", p=P)).then_inc(s_setw, 16)
            sp.dma_start(woutt_sb, woutt).then_inc(s_setw, 16)
            sp.wait_ge(const_ready, 1)
            for dram in (xn_dram, x1_dram, out):
                sp.dma_start(dram[L:ROWS, :], zeros).then_inc(pads_out, 16)
            def load_w2(q):
                sp.dma_start(w2_raw[:, q * NT // 4:(q + 1) * NT // 4, :], w2[q * E // 4:(q + 1) * E // 4].rearrange("e (c p) d -> p (e c) d", p=P)).then_inc(s_w2[q], 16)

            for e in range(E):
                b, m = e % 2, e // 2
                if m > 0:
                    sp.wait_ge(w12_in[b], 16 * m)
                sp.wait_ge(xn_out[b], 16 * m + 16)
                sp.dma_start(w12_raw[:, e * DC:(e + 1) * DC, :], w12[e].rearrange("(c p) i -> p c i", p=P)).then_inc(w12_in[b], 16)
                if e == 3:
                    load_w2(0)
            for q in (1, 2):
                load_w2(q)
            for k in range(W2_PIECES):
                if k < W2_POOL:
                    sp.wait_ge(w2_lo_pool, k + 1)
                else:
                    sp.wait_ge(w2_lo_dve, k - W2_POOL + 1)
                sp.dma_start(w2_lo_dram[:, k * 2 * D:(k + 1) * 2 * D], w2_piece[k % 4]).then_inc(w2_lo_out[k % 4], 16)
                if k == 3:
                    load_w2(3)
            sp.dma_start(x1_dram[0:L, :].rearrange("(p t) d -> p (t d)", p=P), x.rearrange("(p t) d -> p (t d)", p=P)).then_inc(x1_out, 16)
            for b in range(4):
                sp.wait_ge(w2_lo_out[b], 16 * (W2_PIECES // 4))
            sp.dma_start(inw_sb[:], in_wt.rearrange("(c p) n -> p c n", p=P)).then_inc(s_attw, 16)
            sp.dma_start(outw_sb[:], out_wt.rearrange("(c p) n -> p c n", p=P)).then_inc(s_attw, 16)
            sp.dma_start(outb_sb[:], out_b.to_broadcast([P, D])).then_inc(s_attw, 16)

            def load_w2_lo(r, e, b):
                n = e * 16 + E * 16 * r
                if not (isinstance(n, int) and n == 0):
                    sp.wait_ge(w2_lo_in, n)
                sp.dma_start(w2_lo[:, b * IC:(b + 1) * IC, :].bitcast(F32).rearrange("p c d -> p (c d)"),
                             w2_lo_dram[:, bass.ds(e * IC * D, IC * D)]).then_inc(w2_lo_in, 16)

            def first_w2_lo(r):
                sp.wait_ge(slots_ready, r + 1)
                sp.wait_ge(xg_in[1], (r * PAR[1] + 1) * 16)
                for e in range(2):
                    load_w2_lo(r, e, e)

            def next_w2_lo(r):
                with sp.Fori(0, E // 2 - 1) as j:
                    for b in range(2):
                        used = sp.value_load(tile_ends[0:1, bass.ds(j * 2 + b, 1)], min_val=0, max_val=ET) + (r * ET + 1)
                        sp.wait_ge(ye_done, used)
                        load_w2_lo(r, j * 2 + (b + 2), b)
                sp.wait_ge(w2_lo_in, E * 16 * (r + 1))

            first_w2_lo(0)
            sp.wait_ge(lo11_ready, E)
            sp.wait_ge(lo12_ready, E)
            for e in range(E):
                for b, (lo, dram) in enumerate(((w11_lo, w11_lo_dram), (w12_lo, w12_lo_dram))):
                    sp.dma_start(dram[:, e * DC * I:(e + 1) * DC * I],
                                 lo[:, e * DC:(e + 1) * DC, :].bitcast(F32).rearrange("p k i -> p (k i)")).then_inc(lo_out, 16)
                    sp.wait_ge(lo_out, e * 32 + 16 * (b + 1))
            next_w2_lo(0)

            sp.wait_ge(added, 16 * ET)
            for b in range(2):
                sp.dma_start(xin[b], rows(x1_dram, b)).then_inc(x_in[b], 16)
            with sp.Fori(0, NCH // 2 - 1) as j:
                for b in range(2):
                    sp.wait_ge(norm_ready, j * 2 + (NCH + b + 1))
                    sp.dma_start(xin[b], rows(x1_dram, j * 2 + b + 2)).then_inc(x_in[b], 16)

            for b in range(2):
                sp.wait_ge(norm_ready, 2 * NCH - 1 + b)
                sp.dma_start(xin[b], rows(x1_dram, NCH - 1 - b)).then_inc(x_in[b], 16)
            sp.wait_ge(res_step, 1)
            sp.dma_start(xin[0], rows(x1_dram, NCH - 3)).then_inc(x_in[0], 16)

            def store_x2(i, b, c, ahead):
                sp.wait_ge(x2_ready, i + 1)
                sp.dma_start(rows(out, c), x2[b]).then_inc(x_out[b], 16)
                if ahead is not None:
                    sp.wait_ge(res_step, i + 2)
                    sp.dma_start(xin[1 - b], rows(x1_dram, ahead)).then_inc(x_in[1 - b], 16)
                sp.wait_ge(norm_ready, i + (2 * NCH + 1))
                sp.dma_start(rows(xn_dram, c), xn[b]).then_inc(xn_out[b], 16)

            with sp.Fori(0, NCH // 2 - 2) as j:
                for b in range(2):
                    store_x2(j * 2 + b, b, j * -2 + (NCH - 1 - b), j * -2 + (NCH - 4 - b))
            store_x2(NCH - 4, 0, 3, 0)
            for i in range(NCH - 3, NCH):
                store_x2(i, i % 2, NCH - 1 - i, None)
            for b in range(2):
                sp.wait_ge(xn_out[b], 16 * NCH)
                sp.wait_ge(x_out[b], 16 * (NCH // 2))
            sp.wait_ge(states_in, NCH)
            sp.dma_start(w11_lo.bitcast(F32).rearrange("p k i -> p (k i)"), w11_lo_dram).then_inc(lo_in, 16)
            sp.wait_ge(yg_ready, NCH)
            sp.dma_start(w12_lo.bitcast(F32).rearrange("p k i -> p (k i)"), w12_lo_dram).then_inc(lo_in, 16)
            first_w2_lo(1)
            next_w2_lo(1)
            sp.wait_ge(pads_out, 48)
            for b in range(2):
                sp.wait_ge(x_out[b], 16 * (NCH // 2))
                sp.wait_ge(xn_out[b], 16 * NCH)
            sp.wait_ge(added, 2 * 16 * ET)

        @block.gpsimd
        def _(pool):
            step = 0
            def link(ins):
                nonlocal step
                step += 1
                ins.then_inc(pool_const, 1)
                pool.wait_ge(pool_const, step)

            nc.gpsimd.memset(zeros, 0.0)
            nc.gpsimd.memset(neg_half[:], -0.5)
            nc.gpsimd.memset(ln_eps[:], LN_EPS)
            nc.gpsimd.memset(ssm[:, ONE:ONE + 1], 1.0)
            link(nc.gpsimd.memset(ident[:], 0.0))
            nc.gpsimd.affine_select(out=ident[:], in_=ident[:], compare_op=ALU.not_equal, fill=1.0, base=0,
                                    pattern=[[-1, P]], channel_multiplier=1)
            link(nc.gpsimd.iota(iota_i[:], pattern=[[1, P]], base=0, channel_multiplier=0))
            link(nc.gpsimd.tensor_copy(iota_row[:], iota_i[:]))
            link(nc.gpsimd.iota(iota_i[:, 0:E], pattern=[[-1, E]], base=E, channel_multiplier=0))
            link(nc.gpsimd.tensor_copy(e_rank[:], iota_i[:, 0:E]))
            link(nc.gpsimd.iota(iota_i[:, 0:1], pattern=[[1, 1]], base=L + 1, channel_multiplier=1))
            link(nc.gpsimd.tensor_copy(pad_id[:], iota_i[:, 0:1]))
            link(nc.gpsimd.iota(iota_i[:, 0:NQ], pattern=[[P, NT], [0, TOPK]], base=1, channel_multiplier=1))
            nc.gpsimd.tensor_copy(tok_id[:].rearrange("p t k -> p (t k)"), iota_i[:, 0:NQ]).then_inc(const_ready, 1)

            def rsqrt_ln(k, b):
                pool.wait_ge(mv_ready, k + 1)
                nc.gpsimd.tensor_tensor(vars_[:, b, 0, :], mv[:, b, :, 1], ln_eps[:], ALU.add).then_inc(rstd_step, 1)
                pool.wait_ge(rstd_step, k + 1)
                nc.gpsimd.tensor_tensor(rstd[:, b, 0, :], vars_[:, b, 0, :], neg_half[:], ALU.pow).then_inc(rstd_ready, 1)

            def rsqrt_rms(i, b):
                k = i + NCH
                pool.wait_ge(mv_ready, k + 1)
                nc.gpsimd.tensor_copy(x1_mean[:, bass.ds(i * G, G)], mv[:, b, :, 0])
                nc.gpsimd.tensor_tensor(vars_[:, b, 0, :], mv[:, b, :, 1], ln_eps[:], ALU.add).then_inc(kept, 1)
                nc.gpsimd.tensor_scalar(vars_[:, b, 1, :], mv[:, b, :, 1], 1.0 + RMS_EPS, LN_EPS * RMS_EPS, ALU.mult, ALU.add).then_inc(rstd_step, 1)
                pool.wait_ge(rstd_step, k + 1)
                nc.gpsimd.tensor_tensor(rstd[:, b, 1, :], vars_[:, b, 1, :], neg_half[:], ALU.pow).then_inc(rstd_ready, 1)
                pool.wait_ge(kept, i * 2 + 1)
                nc.gpsimd.tensor_tensor(x1_rstd[:, bass.ds(i * G, G)], vars_[:, b, 0, :], neg_half[:], ALU.pow).then_inc(kept, 1)

            def residual(i, m, b):
                pool.wait_ge(t_ready, i + 1)
                if not isinstance(m, int):
                    pool.wait_ge(x_out[b], m * 16)
                    pool.wait_ge(norm_ready, i + (2 * NCH - 1))
                nc.gpsimd.tensor_tensor(x2[b], xin[b], t_rows[b], ALU.add).then_inc(res_step, 1)
                pool.wait_ge(res_step, i + 1)
                nc.gpsimd.tensor_tensor(x2[b], x2[b], outb_sb[:].unsqueeze(1).to_broadcast([P, G, D]), ALU.add).then_inc(res_ready, 1)

            def route_consts(r):
                if r == 0:
                    pool.wait_ge(wct_ready, 1)
                else:
                    pool.wait_ge(o_done, NCH)
                nc.gpsimd.memset(before, 1.0)
                nc.gpsimd.memset(ones, 1.0)
                link(nc.gpsimd.memset(seg, 1.0))
                nc.gpsimd.affine_select(out=before, in_=before, compare_op=ALU.is_gt, fill=0.0, base=0,
                                        pattern=[[1, P]], channel_multiplier=-1)
                nc.gpsimd.memset(seg[:, :, 0], 0.0).then_inc(route_const, 1)

            def id_onehots(r):
                with pool.Fori(0, NQB // 4) as j:
                    for b in range(4):
                        s = j * 4 + b
                        pool.wait_ge(oh_ready, s + (r * NQB + 1))
                        ids = tok_id[:].rearrange("p t k -> p (t k)")[:, bass.ds(s * QB, QB)].unsqueeze(2)
                        nc.gpsimd.tensor_tensor(oha[b][:, :, 0, :], eqa[b], ids.to_broadcast([P, QB, ET]), ALU.mult).then_inc(id_ready, 1)

            def experts(r):
                base = r * ET

                def gather(t, p):
                    done = t + (base - 1)
                    pool.wait_ge(xg_tr, done)
                    nc.gpsimd.tensor_copy(idx_g[p][:], idx_i[:, bass.ds(t, 1)]).then_inc(gather_idx, 1)
                    pool.wait_ge(pads_out, 48)
                    pool.wait_ge(gather_idx, done)
                    nc.gpsimd.indirect_dma_start(xg[p], None, xn_dram, bass.IndirectOffsetOnAxis(ap=idx_g[p][:], axis=0)).then_inc(xg_in[p], 16)

                def scatter(t, p, first=False):
                    done = t + (base + 1)
                    pool.wait_ge(ye_ready, done)
                    if not (first and r == 0):
                        pool.wait_ge(added, t * 16 + 16 * base)
                    nc.gpsimd.tensor_copy(idx_s[:], idx_i[:, bass.ds(t, 1)]).then_inc(scatter_idx, 1)
                    dst = x1_dram if r == 0 else out
                    pool.wait_ge(pads_out, 48)
                    pool.wait_ge(scatter_idx, done)
                    nc.gpsimd.indirect_dma_start(dst, bass.IndirectOffsetOnAxis(ap=idx_s[:], axis=0), yb[p], None,
                                                 compute_op=ALU.add).then_inc(added, 16)

                pool.wait_ge(slots_ready, r + 1)
                for b in range(2):
                    pool.wait_ge(xn_out[b], 16 * (NCH // 2) * (r + 1))
                pool.wait_ge(pads_out, 48)
                if r == 0:
                    pool.wait_ge(x1_out, 16)
                else:
                    for b in range(2):
                        pool.wait_ge(x_out[b], 16 * (NCH // 2))
                for t in range(2):
                    copy = nc.gpsimd.tensor_copy(idx_g[t][:], idx_i[:, t:t + 1])
                    if r == 0:
                        link(copy)
                    else:
                        copy.then_inc(gather_idx, 1)
                        pool.wait_ge(gather_idx, base - 1 + t)
                    nc.gpsimd.indirect_dma_start(xg[t], None, xn_dram, bass.IndirectOffsetOnAxis(ap=idx_g[t][:], axis=0)).then_inc(xg_in[t], 16)
                for t in range(2, 5):
                    gather(t, t % 2)
                scatter(0, 0, first=True)
                with pool.Fori(0, (ET - 5) // 2) as h:
                    for p in range(2):
                        gather(h * 2 + (5 + p), 1 - p)
                        scatter(h * 2 + (1 + p), 1 - p)
                for t in range(ET - 4, ET):
                    scatter(t, t % 2)

            def low_part(e):
                k = slice(e * DC, (e + 1) * DC)
                pool.wait_ge(hi12_ready, e + 1)
                nc.gpsimd.tensor_tensor(w12_lo[:, k, :], w12_raw[:, k, :], w12_hi[:, k, :].bitcast(F32), ALU.subtract).then_inc(lo12_ready, 1)

            def low_w2(k):
                pool.wait_ge(w2_hi_ready, k + 1)
                nc.gpsimd.tensor_tensor(w2_piece[k % 4], w2_piece[k % 4], w2_hi[:, 2 * k:2 * k + 2, :].bitcast(F32).rearrange("p c d -> p (c d)"),
                                        ALU.subtract).then_inc(w2_lo_pool, 1)

            for k in range(NCH):
                rsqrt_ln(k, k % 2)
                if k >= 4:
                    low_part(k - 4)
            route_consts(0)
            for e in range(NCH - 4, NCH - 2):
                low_part(e)
            for k in range(2):
                low_w2(k)
            for e in range(NCH - 2, E):
                low_part(e)
            for k in range(2, W2_POOL):
                low_w2(k)
            id_onehots(0)
            experts(0)
            with pool.Fori(0, NCH // 2) as j:
                for b in range(2):
                    rsqrt_rms(j * 2 + b, b)
            pool.wait_ge(s_attw, 48)
            for b in range(2):
                residual(b, 0, b)
            with pool.Fori(0, NCH // 2 - 1) as j:
                for b in range(2):
                    rsqrt_ln(j * 2 + (b + 2 * NCH), b)
                    residual(j * 2 + (b + 2), j + 1, b)
            for b in range(2):
                rsqrt_ln(3 * NCH - 2 + b, b)
            route_consts(1)
            id_onehots(1)
            experts(1)

        @block.scalar
        def _(act):
            act.dma_start(col[:], cols).then_inc(s_cols, 16)
            act.wait_ge(s_cols, 16)
            nc.scalar.activation(ssm[:, EXPA:EXPA + 1], col[:, C_LOGA:C_LOGA + 1], ACT.Exp).then_inc(ssm_exp, 1)
            nc.scalar.activation(ssm[:, DT:DT + 1], col[:, C_LOGDT:C_LOGDT + 1], ACT.Exp).then_inc(ssm_exp, 1)
            act.wait_ge(ssm_step, 2)
            nc.scalar.activation(ssm[:, ABAR:ABAR + 1], ssm[:, ADT:ADT + 1], ACT.Exp).then_inc(ssm_exp, 1)

            def rows_t(k, b):
                act.wait_ge(tr_done, k + 1)
                for h in range(DC):
                    last = nc.scalar.activation(xnt[b][:, h, :], ps_t[h][:], ACT.Copy)
                last.then_inc(xnt_ready, 1)

            def logits_out(n, c):
                act.wait_ge(logits_done, n + 1)
                nc.scalar.activation(logits[:, bass.ds(c * G, G), :].rearrange("p t e -> p (t e)"), ps_l[:, 0:G * E], ACT.Copy).then_inc(logits_copied, 1)

            def load_table(function):
                nc.scalar.activation(table[:], ssm[:, ONE:ONE + 1], function)

            def split_w2(pieces):
                for k in pieces:
                    b, m = k % 4, k // 4
                    act.wait_ge(s_w2[m], 16)
                    if m == 0:
                        act.wait_ge(pads_out, 48)
                    else:
                        act.wait_ge(w2_lo_out[b], m * 16)
                    split_w2_piece(k, b)

            def split_w2_piece(k, b):
                rows_k = w2_raw[:, 2 * k:2 * k + 2, :].rearrange("p c d -> p (c d)")
                nc.scalar.activation(w2_piece[b], rows_k, ACT.Copy)
                nc.scalar.activation(w2_hi[:, 2 * k:2 * k + 2, :].rearrange("p c d -> p (c d)"), rows_k, ACT.Copy).then_inc(w2_hi_ready, 1)

            def router_exp(r):
                act.wait_ge(route_step, r * RS + 2)
                nc.scalar.activation(R[1], R[0], ACT.Exp).then_inc(route_exp, 1)
                load_table(ACT.Sigmoid)
                if r == 0:
                    high_w12(NCH - 1, NCH // 2 - 1, 1)
                    split_w2(range(2, W2_PIECES))
                scores = tok[1].rearrange("p t k -> p (t k)")
                with act.Fori(0, NQB // 4) as j:
                    for b in range(4):
                        s = j * 4 + b
                        act.wait_ge(oh_ready, s + (r * NQB + 1))
                        for q in range(QB):
                            last = nc.scalar.activation(oha[b][:, q, 1, :], eqa[b][:, q, :], ACT.Copy, scale=scores[:, bass.ds(s * QB + q, 1)])
                        last.then_inc(score_ready, 1)

            def experts(r):
                base = r * ET

                def hidden_high(t, p):
                    act.wait_ge(f_tr, t + (base + 1))
                    if not (isinstance(t, int) and t < 2):
                        act.wait_ge(ye_done, t + base)
                    nc.scalar.activation(ft_hi[p].rearrange("p c k -> p (c k)"), ps_f[:], ACT.Copy).then_inc(ft_hi_ready, 1)

                def output(t, p):
                    act.wait_ge(ye_done, t + (base + 2))
                    if not (isinstance(t, int) and t < 2):
                        act.wait_ge(added, t * 16 + 16 * (base - 1))
                    nc.scalar.activation(yb[p], ps_u[:, 0:D], ACT.Copy, scale=w_slot[:, bass.ds(t, 1)]).then_inc(ye_ready, 1)

                def tile(t, p):
                    early = t if isinstance(t, int) else ET
                    act.wait_ge(g_done, t + (base + 1))
                    if early > 1:
                        act.wait_ge(f_step, t + (base - 1))
                    nc.scalar.activation(sg[p], ps_g[p][:], ACT.Sigmoid).then_inc(sg_ready, 1)
                    if early > 0:
                        hidden_high(t - 1, 1 - p)
                    if early > 1:
                        output(t - 2, p)

                act.wait_ge(slots_ready, r + 1)
                for t in range(5):
                    tile(t, t % 2)
                with act.Fori(0, (ET - 5) // 2) as h:
                    tile(h * 2 + 5, 1)
                    tile(h * 2 + 6, 0)
                hidden_high(ET - 1, (ET - 1) % 2)
                for t in range(ET - 2, ET):
                    output(t, t % 2)

            def load_w11(e, b):
                k = bass.ds(e * DC, DC)
                act.dma_start(w11_raw[:, k, :], w11[bass.ds(e, 1)].rearrange("e (c p) i -> p (e c) i", p=P)).then_inc(w11_in[b], 16)

            def high_w11(e, m, b):
                k = bass.ds(e * DC, DC)
                act.wait_ge(w11_in[b], m * 16 + 16)
                nc.scalar.activation(w11_hi[:, k, :], w11_raw[:, k, :], ACT.Copy).then_inc(hi11_ready, 1)

            def high_w12(e, m, b):
                k = bass.ds(e * DC, DC)
                act.wait_ge(w12_in[b], m * 16 + 16)
                nc.scalar.activation(w12_hi[:, k, :], w12_raw[:, k, :], ACT.Copy).then_inc(hi12_ready, 1)

            def rows_out(k, b):
                act.dma_start(rows(xn_dram, k), xn[b]).then_inc(xn_out[b], 16)

            def chunk(k, m, b):
                rows_t(k, 1 - b)
                rows_out(k, 1 - b)
                high_w11(k - 1, m, b)
                load_w11(k + 1, b)
                logits_out(k - 1, k - 1)

            rows_t(0, 0)
            rows_out(0, 0)
            load_w11(0, 0)
            load_w11(1, 1)
            for k in (1, 2):
                chunk(k, 0, k - 1)
            high_w12(0, 0, 0)
            with act.Fori(0, (NCH - 4) // 2) as j:
                for b in range(2):
                    chunk(j * 2 + (b + 3), j + 1, b)
                    high_w12(j * 2 + (b + 1), j + b, 1 - b)
            rows_t(NCH - 1, 1)
            rows_out(NCH - 1, 1)
            high_w11(NCH - 2, NCH // 2 - 1, 0)
            logits_out(NCH - 2, NCH - 2)
            high_w12(NCH - 3, NCH // 2 - 2, 1)
            high_w11(NCH - 1, NCH // 2 - 1, 1)
            split_w2(range(2))
            logits_out(NCH - 1, NCH - 1)
            high_w12(NCH - 2, NCH // 2 - 1, 0)
            router_exp(0)
            experts(0)

            def project(i, last):
                i2, b = i
                for jc in range(2 * DC):
                    if jc == DC and not last:
                        rows_t(i2 + (NCH + 1), 1 - b)
                    act.wait_ge(proj_done, i2 * (2 * DC) + (jc + 1))
                    if jc < DC:
                        nc.scalar.activation(seq[:, jc, bass.ds(i2 * CH + 2, CH)], ps_p[jc][:], ACT.Identity,
                                             bias=col[:, C_INB + jc:C_INB + jc + 1]).then_inc(xz_ready, 1)
                    else:
                        nc.scalar.activation(gate[:, jc - DC, bass.ds(i2 * CH, CH)], ps_p[jc][:], ACT.Sigmoid,
                                             bias=col[:, C_INB + jc:C_INB + jc + 1]).then_inc(xz_ready, 1)

            rows_t(NCH, 0)
            with act.Fori(0, NCH // 2 - 1) as j:
                for b in range(2):
                    project((j * 2 + b, b), False)
            project((NCH - 2, 0), False)
            project((NCH - 1, 1), True)

            def take_states(i, b, c):
                nc.scalar.activation(states[:, b, :], seq[:, 0, bass.ds(c * CH + 1, CH)], ACT.Copy).then_inc(states_in, 1)

            def norm_t(i, m, b, c):
                if not (isinstance(i, int) and i < 2):
                    act.wait_ge(res_step, i - 1)
                act.wait_ge(x_in[b], m * 16 + 16 * (NCH + 1))
                for t in range(G):
                    last = nc.scalar.activation(t_rows[b][:, t, :], xin[b][:, t, :], ACT.Identity, bias=x1_mean[:, bass.ds(c * G + t, 1)])
                last.then_inc(t_step, 1)
                act.wait_ge(t_step, i + 1)
                for t in range(G):
                    last = nc.scalar.activation(t_rows[b][:, t, :], t_rows[b][:, t, :], ACT.Copy, scale=x1_rstd[:, bass.ds(c * G + t, 1)])
                last.then_inc(t_ready, 1)

            def states_ahead(i, b, c):
                act.wait_ge(y_done, i - 1)
                act.wait_ge(bwd_done, i + 1)
                take_states(i, b, c)

            load_table(ACT.Exp)
            act.wait_ge(neg_mean, 1)
            norm_t(0, 0, 0, NCH - 1)
            act.wait_ge(fwd_done, NCH + 1)
            act.wait_ge(bwd_done, 1)
            take_states(0, 0, NCH - 1)
            norm_t(1, 0, 1, NCH - 2)
            act.wait_ge(bwd_done, 2)
            take_states(1, 1, NCH - 2)
            norm_t(2, 1, 0, NCH - 3)
            states_ahead(2, 0, NCH - 3)
            states_ahead(3, 1, NCH - 4)
            norm_t(3, 1, 1, NCH - 4)
            rows_t(2 * NCH, 0)
            with act.Fori(0, NCH // 2 - 2) as j:
                for b in range(2):
                    i = j * 2 + (b + 2)
                    states_ahead(j * 2 + (b + 4), b, j * -2 + (NCH - 5 - b))
                    norm_t(j * 2 + (b + 4), j + 2, b, j * -2 + (NCH - 5 - b))
                    logits_out(j * 2 + (b + NCH), j * -2 + (NCH - 1 - b))
                    rows_t(i + (2 * NCH - 1), 1 - b)
            for i in range(NCH - 2, NCH + 1):
                logits_out(i + NCH - 2, NCH + 1 - i)
                rows_t(i + 2 * NCH - 1, (i - 1) % 2)
            logits_out(2 * NCH - 1, 0)
            router_exp(1)
            experts(1)

        @block.vector
        def _(dve):
            def chain(sem_, start):
                at = [start]

                def link(ins, wait=True):
                    at[0] += 1
                    ins.then_inc(sem_, 1)
                    if wait:
                        dve.wait_ge(sem_, at[0])
                return link, at

            link, at = chain(ssm_step, 0)
            v = lambda k: ssm[:, k:k + 1]
            dve.wait_ge(const_ready, 1)
            dve.wait_ge(ssm_exp, 2)
            link(nc.vector.tensor_scalar(v(AA), v(EXPA), -1.0, None, ALU.mult))
            link(nc.vector.tensor_tensor(v(ADT), v(AA), v(DT), ALU.mult))
            nc.vector.tensor_scalar(a_mask[:], v(EXPA), A_EPS, None, ALU.is_lt)
            link(nc.vector.tensor_copy(v(DEN), v(AA)))
            link(nc.vector.copy_predicated(v(DEN), a_mask[:], v(ONE)))
            link(nc.vector.reciprocal(v(RDEN), v(DEN)))
            dve.wait_ge(ssm_exp, 3)
            link(nc.vector.tensor_scalar(v(FRAC), v(ABAR), -1.0, v(RDEN), ALU.add, ALU.mult))
            link(nc.vector.copy_predicated(v(FRAC), a_mask[:], v(DT)))
            link(nc.vector.tensor_tensor(v(BBAR), v(FRAC), col[:, C_B:C_B + 1], ALU.mult))
            def rows_of(b):
                return lambda t: xin[b][:, t, :]

            def ln_stats(k, b, src):
                for t in range(G):
                    last = nc.vector.bn_stats(bnst[:, b, t, :], src(t))
                last.then_inc(ln_step, 1)
                dve.wait_ge(ln_step, k + 1)
                nc.vector.memset(fence[:], 0.0)
                for t in range(G):
                    last = nc.vector.bn_aggr(mv[:, b, t, :], bnst[:, b, t, :])
                last.then_inc(mv_ready, 1)

            def ln_apply(k, b, src, which=0):
                dve.wait_ge(rstd_ready, k + 1)
                for t in range(G):
                    last = nc.vector.tensor_scalar(xn[b][:, t, :], src(t), mv[:, b, t, 0:1], rstd[:, b, which, t:t + 1], ALU.subtract, ALU.mult)
                last.then_inc(norm_ready, 1)

            def router(r):
                link, at = chain(route_step, r * RS)
                grid = lambda a: a.rearrange("p (t e) -> p t e", e=E)
                cols_ = lambda a: a.rearrange("p (e t) -> p e t", e=E)
                flip = lambda a: a.rearrange("p (e t) -> p t e", e=E)
                over_e = lambda a: a.unsqueeze(2).to_broadcast([P, NT, E])
                rank = e_rank[:].unsqueeze(1).to_broadcast([P, NT, E])
                lg = logits[:]
                s0, s1, s2, s3 = (small[:, k * NT:(k + 1) * NT] for k in range(4))
                best = [tok[0][:, :, k] for k in range(TOPK)]
                dve.wait_ge(route_const, r + 1)
                dve.wait_ge(logits_copied, NCH * (r + 1))
                for b in range(2):
                    dve.wait_ge(xn_out[b], 16 * (NCH // 2) * (r + 1))
                    if r == 1:
                        dve.wait_ge(x_out[b], 16 * (NCH // 2))
                link(nc.vector.reduce_max(s0, lg, AX.X))
                link(nc.vector.tensor_tensor(grid(R[0]), lg, over_e(s0), ALU.subtract))
                dve.wait_ge(route_exp, r + 1)
                link(nc.vector.reduce_sum(s1, grid(R[1]), AX.X))
                link(nc.vector.reciprocal(s2, s1))
                link(nc.vector.tensor_tensor(grid(R[2]), grid(R[1]), over_e(s2), ALU.mult))
                onehot = [R[5], R[8]]
                prob = R[2]
                for k in range(TOPK):
                    link(nc.vector.reduce_max(best[k], grid(prob), AX.X))
                    link(nc.vector.tensor_tensor(grid(R[3]), grid(prob), over_e(best[k]), ALU.is_equal))
                    link(nc.vector.tensor_tensor(grid(R[4]), grid(R[3]), rank, ALU.mult))
                    link(nc.vector.reduce_max(s3, grid(R[4]), AX.X))
                    link(nc.vector.tensor_tensor(flip(onehot[k]), over_e(s3), rank, ALU.is_equal))
                    if k == 0:
                        link(nc.vector.scalar_tensor_tensor(grid(R[6]), flip(onehot[0]), -2.0, grid(prob), ALU.mult, ALU.add))
                        prob = R[6]
                link(nc.vector.tensor_tensor(R[9], onehot[0], onehot[1], ALU.add))
                link(nc.vector.tensor_tensor(s0, best[0], best[1], ALU.add))
                link(nc.vector.tensor_scalar(s1, s0, SUM_EPS, None, ALU.add))
                link(nc.vector.reciprocal(s2, s1))
                for k in range(TOPK):
                    last = nc.vector.scalar_tensor_tensor(tok[1][:, :, k], best[k], 0.5, s2, ALU.mult, ALU.mult)
                link(last)
                cnt, tiles_i, tiles, ends, first = (small[:, 128 + 8 * k:136 + 8 * k] for k in range(5))
                dve.wait_ge(ranks_done, r + 1)
                rank_ps, tot_ps = ps_u[:, 0:NT * E], ps_u[:, NT * E:2 * NT * E]
                link(nc.vector.tensor_copy(R[0], tot_ps))
                nc.vector.reduce_sum(cnt, cols_(R[0]), AX.X)
                link(nc.vector.tensor_tensor_scan(R[1], seg.rearrange("p e t -> p (e t)"), R[0], 0.0, ALU.mult, ALU.add))
                link(nc.vector.tensor_scalar(tiles_i.bitcast(I32), cnt, float(P - 1), None, ALU.add))
                link(nc.vector.tensor_scalar(tiles_i.bitcast(I32), tiles_i.bitcast(I32), 7, None, ALU.logical_shift_right))
                link(nc.vector.tensor_copy(tiles, tiles_i.bitcast(I32)))
                link(nc.vector.tensor_tensor_scan(ends, ones[:, 0:E], tiles, 0.0, ALU.mult, ALU.add))
                link(nc.vector.tensor_tensor(first, ends, tiles, ALU.subtract))
                link(nc.vector.tensor_tensor(R[1], R[1], R[0], ALU.subtract))
                link(nc.vector.tensor_tensor(R[2], rank_ps, R[1], ALU.add))
                link(nc.vector.scalar_tensor_tensor(cols_(R[3]), first.unsqueeze(2).to_broadcast([P, E, NT]), float(P), cols_(R[2]), ALU.mult, ALU.add))
                for k in range(TOPK):
                    last = nc.vector.tensor_tensor([R[4], R[7]][k], onehot[k], R[3], ALU.mult)
                link(last)
                for k in range(TOPK):
                    last = nc.vector.reduce_sum(tok[2][:, :, k], flip([R[4], R[7]][k]), AX.X)
                link(last)
                flat = lambda a: a.rearrange("p t k -> p (t k)")
                link(nc.vector.tensor_copy(flat(tok[3]).bitcast(I32), flat(tok[2])))
                nc.vector.tensor_scalar(flat(tok[4]).bitcast(I32), flat(tok[3]).bitcast(I32), P - 1, None, ALU.bitwise_and)
                link(nc.vector.tensor_scalar(flat(tok[5]).bitcast(I32), flat(tok[3]).bitcast(I32), 7, None, ALU.logical_shift_right))
                nc.vector.tensor_copy(flat(tok[6]), flat(tok[4]).bitcast(I32))
                link(nc.vector.tensor_copy(flat(tok[7]), flat(tok[5]).bitcast(I32)))
                ob = r * NQB

                def onehots(s, b, free):
                    if free:
                        dve.wait_ge(inv_used, s + (ob - 3))
                    q = bass.ds(s * QB, QB)
                    place, tile_ = (flat(a)[:, q].unsqueeze(2) for a in (tok[6], tok[7]))
                    nc.vector.tensor_tensor(ohb[b], iota_row[:].unsqueeze(1).to_broadcast([P, QB, P]), place.to_broadcast([P, QB, P]), ALU.is_equal)
                    nc.vector.tensor_tensor(eqa[b], iota_row[:, 0:ET].unsqueeze(1).to_broadcast([P, QB, ET]), tile_.to_broadcast([P, QB, ET]), ALU.is_equal).then_inc(oh_ready, 1)

                for s in range(4):
                    onehots(s, s, False)
                link(nc.vector.tensor_tensor(past_end, iota_row[:, 0:ET].unsqueeze(2).to_broadcast([P, ET, E - 1]),
                                             ends[:, 0:E - 1].unsqueeze(1).to_broadcast([P, ET, E - 1]), ALU.is_ge))
                link(nc.vector.reduce_sum(past_ends, past_end, AX.X))
                nc.vector.tensor_copy(tile_ends[:], ends)
                nc.vector.tensor_copy(eid[:, 0:2], past_ends[:, 0:2])
                nc.vector.scalar_tensor_tensor(eid[:, 2:ET], past_ends[:, 0:ET - 2], float(E), past_ends[:, 2:ET], ALU.mult, ALU.add)
                link(nc.vector.tensor_scalar(eid[:, ET:ET + 2], past_ends[:, ET - 2:ET], float(E), None, ALU.mult))
                if r == 0:
                    for k in range(W2_POOL, W2_PIECES):
                        dve.wait_ge(w2_hi_ready, k + 1)
                        nc.vector.tensor_tensor(w2_piece[k % 4], w2_piece[k % 4], w2_hi[:, 2 * k:2 * k + 2, :].bitcast(F32).rearrange("p c d -> p (c d)"),
                                                ALU.subtract).then_inc(w2_lo_dve, 1)
                with dve.Fori(0, NQB // 4 - 1) as j:
                    for b in range(4):
                        onehots(j * 4 + (4 + b), b, True)
                dve.wait_ge(inv_done, r + 1)
                inv_id, inv_w = ps_l[:, 0:ET], ps_l[:, ET:2 * ET]
                nc.vector.tensor_copy(w_slot[:], inv_w)
                link(nc.vector.tensor_scalar(R[2][:, 0:ET], inv_id, 0.0, pad_id[:], ALU.is_equal, ALU.mult))
                nc.vector.scalar_tensor_tensor(idx_i[:], inv_id, -1.0, R[2][:, 0:ET], ALU.add, ALU.add).then_inc(slots_ready, 1)
                dve.wait_ge(slots_ready, r + 1)
                assert at[0] == (r + 1) * RS, at[0] - r * RS

            def experts(r):
                base = r * ET

                def rows_in(t, p):
                    dve.wait_ge(xg_tr, t + (base + 1))
                    hi, lo = (a[p].rearrange("p c k -> p (c k)") for a in (xt_hi, xt_lo))
                    nc.vector.tensor_copy(hi, ps_x[:, 0:D]).then_inc(xt_step, 1)
                    dve.wait_ge(xt_step, t + (base + 1))
                    nc.vector.tensor_tensor(lo, ps_x[:, 0:D], hi.bitcast(F32), ALU.subtract).then_inc(xt_ready, 1)

                def hidden_low(t, p):
                    dve.wait_ge(ft_hi_ready, t + (base + 1))
                    hi, lo = (a[p].rearrange("p c k -> p (c k)") for a in (ft_hi, ft_lo))
                    nc.vector.tensor_tensor(lo, ps_f[:], hi.bitcast(F32), ALU.subtract).then_inc(ft_ready, 1)

                def tile(t, p, first=False, last=False):
                    dve.wait_ge(sg_ready, t + (base + 1))
                    nc.vector.tensor_tensor(sg[p], sg[p], ps_g[p][:], ALU.mult).then_inc(f_step, 1)
                    if not first:
                        hidden_low(t - 1, 1 - p)
                    if not last:
                        rows_in(t + 1, 1 - p)
                    dve.wait_ge(f_step, t + (base + 1))
                    dve.wait_ge(v_done, t + (base + 1))
                    nc.vector.tensor_tensor(fu[p], sg[p], ps_v[p][:], ALU.mult).then_inc(f_ready, 1)

                rows_in(0, 0)
                tile(0, 0, first=True)
                with dve.Fori(0, ET // 2 - 1) as h:
                    tile(h * 2 + 1, 1)
                    tile(h * 2 + 2, 0)
                tile(ET - 2, 1)
                tile(ET - 1, 0, last=True)
                hidden_low(ET - 1, 0)

            def stats_x(k, j, b):
                dve.wait_ge(x_in[b], j * 16 + 16)
                ln_stats(k, b, x_of(k))

            def x_of(k):
                return lambda t: x_all[:, bass.ds(k * G + t, 1), :].rearrange("p a d -> p (a d)")

            def norm_x(k, j, b):
                dve.wait_ge(tr_done, k - 1)
                dve.wait_ge(xn_out[b], j * 16)
                ln_apply(k, b, x_of(k))

            def low_part(e):
                k = bass.ds(e * DC, DC)
                dve.wait_ge(hi11_ready, e + 1)
                nc.vector.tensor_tensor(w11_lo[:, k, :], w11_raw[:, k, :], w11_hi[:, k, :].bitcast(F32), ALU.subtract).then_inc(lo11_ready, 1)

            for k in range(2):
                stats_x(k, 0, k)
            ln_apply(0, 0, x_of(0))
            stats_x(2, 1, 0)
            ln_apply(1, 1, x_of(1))
            stats_x(3, 1, 1)
            norm_x(2, 1, 0)
            with dve.Fori(0, NCH // 2 - 2) as j:
                for b in range(2):
                    stats_x(j * 2 + (b + 4), j + 2, b)
                    norm_x(j * 2 + (b + 3), j + (b + 1), 1 - b)
                    low_part(j * 2 + b)
            norm_x(NCH - 1, NCH // 2 - 1, 1)
            dve.wait_ge(s_setw, 48)
            dve.wait_ge(s_cols, 16)
            nc.vector.tensor_scalar(woc_sb[:], woutt_sb, col[:, C_C:C_C + 1], None, ALU.mult)
            dve.wait_ge(wct_done, 1)
            nc.vector.tensor_copy(wct_sb[:].rearrange("p c n -> p (c n)"), ps_p[0][:, 0:D])
            nc.vector.tensor_copy(v(UB), ps_p[1][:, 0:1]).then_inc(wct_ready, 1)
            dve.wait_ge(wct_ready, 1)
            for e in range(NCH - 4, E):
                low_part(e)
            router(0)
            experts(0)

            def stats_x1(i, m, b):
                dve.wait_ge(x_in[b], m * 16 + 16 * (NCH // 2 + 1))
                ln_stats(i + NCH, b, rows_of(b))

            def norm_x1(i, b):
                dve.wait_ge(tr_done, i + (NCH - 1))
                ln_apply(i + NCH, b, rows_of(b), 1)

            def convolve(c, b):
                dww = lambda h, k: col[:, C_DWW + 3 * h + k:C_DWW + 3 * h + k + 1]
                last_c = isinstance(c, int) and c == NCH - 1
                dve.wait_ge(xz_ready, NCH * 4 if last_c else c * 4 + (4 + DC))
                to = conv[b]
                for h in range(DC):
                    last = nc.vector.tensor_scalar(to[:, h, :], seq[:, h, bass.ds(c * CH + 2, CH)], dww(h, 1), col[:, C_DWB + h:C_DWB + h + 1], ALU.mult, ALU.add)
                last.then_inc(conv_step, 1)
                dve.wait_ge(conv_step, c * 2 + 1)
                for h in range(DC):
                    last = nc.vector.scalar_tensor_tensor(to[:, h, :], seq[:, h, bass.ds(c * CH + 1, CH)], dww(h, 0), to[:, h, :], ALU.mult, ALU.add)
                last.then_inc(conv_step, 1)
                dve.wait_ge(conv_step, c * 2 + 2)
                for h in range(DC):
                    last = nc.vector.scalar_tensor_tensor(to[:, h, :], seq[:, h, bass.ds(c * CH + 3, CH)], dww(h, 2), to[:, h, :], ALU.mult, ALU.add)
                last.then_inc(conv_ready, 1)

            def scan_forward(c):
                here = seq[:, 0, bass.ds(c * CH + 1, CH)]
                dve.wait_ge(conv_ready, c + 1)
                dve.wait_ge(u_done, c + 1)
                nc.vector.tensor_scalar(here, ps_u[:], v(UB), v(BBAR), ALU.add, ALU.mult).then_inc(u_ready, 1)
                dve.wait_ge(u_ready, c + 2)
                dve.wait_ge(fwd_done, c + 1)
                nc.vector.tensor_tensor_scan(here[0:N], ssm[0:N, ABAR:ABAR + 1].to_broadcast([N, CH]), here[0:N],
                                             seq[0:N, 0, bass.ds(c * CH, 1)], ALU.mult, ALU.add).then_inc(fwd_done, 1)

            dve.wait_ge(lo_out, 32 * E)
            nc.vector.memset(seq[:, :, 0:2], 0.0).then_inc(u_ready, 1)
            nc.vector.memset(seq[:, :, L + 2:L + 3], 0.0).then_inc(fwd_done, 1)
            dve.wait_ge(s_attw, 48)
            for c in range(DC):
                last = nc.vector.tensor_scalar(inw_sb[:, c, :], inw_sb[:, c, :], col[:, C_NS + c:C_NS + c + 1], None, ALU.mult)
            last.then_inc(inw_ready, 1)
            for b in range(2):
                stats_x1(b, 0, b)
            for b in range(2):
                norm_x1(b, b)
            stats_x1(2, 1, 0)
            norm_x1(2, 0)
            stats_x1(3, 1, 1)
            convolve(0, 0)
            norm_x1(3, 1)
            with dve.Fori(0, NCH // 2 - 2) as j:
                for b in range(2):
                    i = j * 2 + (b + 4)
                    stats_x1(i, j + 2, b)
                    convolve(j * 2 + (b + 1), 1 - b)
                    norm_x1(i, b)
                    scan_forward(j * 2 + b)
            for c in range(NCH - 3, NCH):
                convolve(c, c % 2)
                scan_forward(c - 1)

            def scan_backward(i, b):
                dve.wait_ge(states_in, i + 1)
                dve.wait_ge(bwd_done, i + 1)
                back = states[N:P, b, ::-1]
                nc.vector.tensor_tensor_scan(back, ssm[N:P, ABAR:ABAR + 1].to_broadcast([N, CH]), back,
                                             states[N:P, 1 - b, 0:1], ALU.mult, ALU.add).then_inc(bwd_done, 1)

            def gate_y(i, c):
                dve.wait_ge(y_done, i + 1)
                for h in range(DC):
                    last = nc.vector.tensor_tensor(mix[:, h, :], gate[:, h, bass.ds(c * CH, CH)], ps_p[h][:], ALU.mult)
                last.then_inc(yg_ready, 1)

            def add_mixer(i, b):
                dve.wait_ge(res_ready, i + 1)
                dve.wait_ge(o_done, i + 1)
                for h in range(2):
                    half = x2[b][:, 2 * h:2 * h + 2, :].rearrange("p t d -> p (t d)")
                    last = nc.vector.tensor_tensor(half, half, ps_p[2 + h][:], ALU.add)
                last.then_inc(x2_ready, 1)

            def stats_x2(i, b):
                dve.wait_ge(x2_ready, i + 1)
                ln_stats(i + 2 * NCH, b, x2_of(b))

            def x2_of(b):
                return lambda t: x2[b][:, t, :]

            def norm_x2(i, m, b):
                dve.wait_ge(tr_done, i + (2 * NCH - 1))
                dve.wait_ge(xn_out[b], m * 16 + 16 * (NCH // 2))
                ln_apply(i + 2 * NCH, b, x2_of(b))

            dve.wait_ge(kept, 2 * NCH)
            nc.vector.tensor_scalar(x1_mean[:], x1_mean[:], -1.0, None, ALU.mult).then_inc(neg_mean, 1)
            scan_forward(NCH - 1)
            nc.vector.memset(states[N:P, 1, 0:1], 0.0).then_inc(bwd_done, 1)
            scan_backward(0, 0)
            gate_y(0, NCH - 1)
            scan_backward(1, 1)
            with dve.Fori(0, NCH // 2 - 1) as j:
                for b in range(2):
                    i = j * 2 + b
                    add_mixer(i, b)
                    gate_y(i + 1, j * -2 + (NCH - 2 - b))
                    stats_x2(i, b)
                    scan_backward(i + 2, b)
                    norm_x2(i, j, b)
            add_mixer(NCH - 2, 0)
            gate_y(NCH - 1, 0)
            stats_x2(NCH - 2, 0)
            norm_x2(NCH - 2, NCH // 2 - 1, 0)
            add_mixer(NCH - 1, 1)
            stats_x2(NCH - 1, 1)
            norm_x2(NCH - 1, NCH // 2 - 1, 1)
            router(1)
            experts(1)

        @block.tensor
        def _(pe):
            def transposes(k, b):
                pe.wait_ge(norm_ready, k + 1)
                if not (isinstance(k, int) and k == 0):
                    pe.wait_ge(xnt_ready, k)
                for t in range(G):
                    for h in range(DC):
                        last = nc.tensor.transpose(ps_t[h][:, t * P:(t + 1) * P], xn[b][:, t, h * P:(h + 1) * P], ident[:])
                last.then_inc(tr_done, 1)

            def route_chunk(k, n, b):
                pe.wait_ge(xnt_ready, k + 1)
                if not (isinstance(n, int) and n == 0):
                    pe.wait_ge(logits_copied, n)
                for t in range(G):
                    for h in range(DC):
                        last = nc.tensor.matmul(ps_l[:, t * E:(t + 1) * E], xnt[b][:, h, t * P:(t + 1) * P], wg_sb[:, h, :],
                                                start=(h == 0), stop=(h == DC - 1))
                last.then_inc(logits_done, 1)

            def fold():
                pe.wait_ge(s_setw, 48)
                pe.wait_ge(s_cols, 16)
                for dc in range(DC):
                    for ec in range(DC):
                        nc.tensor.matmul(ps_p[0][:, dc * P:(dc + 1) * P], pw_sb[:, ec, dc * P:(dc + 1) * P], wint_sb[:, ec, :],
                                         start=(ec == 0), stop=(ec == DC - 1))
                for ec in range(DC):
                    last = nc.tensor.matmul(ps_p[1][:, 0:1], wint_sb[:, ec, :], col[:, C_PWB + ec:C_PWB + ec + 1], start=(ec == 0), stop=(ec == DC - 1))
                last.then_inc(wct_done, 1)

            def router(r):
                pe.wait_ge(route_step, r * RS + 17)
                mm = nc.tensor.matmul(ps_u[:, 0:NT * E], before, R[9], start=True, stop=True)
                if r == 0:
                    mm.then_inc(ye_done, 1)
                nc.tensor.matmul(ps_u[:, NT * E:2 * NT * E], ones, R[9], start=True, stop=True).then_inc(ranks_done, 1)
                ob = r * NQB

                def invert(s, b, first=False, done=inv_used):
                    pe.wait_ge(id_ready, s + (ob + 1))
                    pe.wait_ge(score_ready, s + (ob + 1))
                    for q in range(QB):
                        last = nc.tensor.matmul(ps_l[:, 0:2 * ET], ohb[b][:, q, :], oha[b][:, q, :, :].rearrange("p a t -> p (a t)"),
                                                start=(first and q == 0), stop=(done is inv_done and q == QB - 1))
                    last.then_inc(done, 1)

                for s in range(4):
                    invert(s, s, first=(s == 0))
                with pe.Fori(0, NQB // 4 - 2) as j:
                    for b in range(4):
                        invert(j * 4 + (4 + b), b)
                for b in range(4):
                    invert(NQB - 4 + b, b, done=inv_done if b == 3 else inv_used)

            def experts(r):
                base = r * ET

                def rows_in(t, h, p):
                    pe.wait_ge(xg_in[p], (h + (r * PAR[p] + 1)) * 16)
                    for c in range(DC):
                        last = nc.tensor.transpose(ps_x[:, c * P:(c + 1) * P], xg[p][:, c * P:(c + 1) * P], ident[:])
                    last.then_inc(xg_tr, 1)

                def up(p, w_hi_sb, w_lo_sb, dst, e, done):
                    for c in range(DC):
                        of = lambda w: w[:, bass.ds(e * DC + c, 1), :].rearrange("p a i -> p (a i)")
                        parts = ((xt_hi, w_hi_sb), (xt_hi, w_lo_sb), (xt_lo, w_hi_sb))
                        for n, (xt, w) in enumerate(parts):
                            last = nc.tensor.matmul(dst[p][:], xt[p][:, c, :], of(w), start=(c == 0 and n == 0),
                                                    stop=(c == DC - 1 and n == len(parts) - 1))
                    last.then_inc(done, 1)

                def hidden_in(t, p):
                    if not (isinstance(t, int) and t == 0):
                        pe.wait_ge(ft_ready, t + base)
                    pe.wait_ge(f_ready, t + (base + 1))
                    for c in range(IC):
                        last = nc.tensor.transpose(ps_f[:, c * P:(c + 1) * P], fu[p][:, c * P:(c + 1) * P], ident[:])
                    last.then_inc(f_tr, 1)

                def down(t, p, e):
                    pe.wait_ge(w2_lo_in, e * 16 + (16 + E * 16 * r))
                    if isinstance(t, int) and t == ET - 1:
                        pe.wait_ge(ft_ready, t + (base + 1))
                    if not (isinstance(t, int) and t == 0):
                        pe.wait_ge(ye_ready, t + base)
                    for c in range(IC):
                        hi = w2_hi[:, bass.ds(e * IC + c, 1), :].rearrange("p a d -> p (a d)")
                        lo = w2_lo[:, bass.ds((e & 1) * IC + c, 1), :].rearrange("p a d -> p (a d)")
                        parts = ((ft_hi, hi), (ft_hi, lo), (ft_lo, hi))
                        for n, (f, w) in enumerate(parts):
                            last = nc.tensor.matmul(ps_u[:, 0:D], f[p][:, c, :], w, start=(c == 0 and n == 0),
                                                    stop=(c == IC - 1 and n == len(parts) - 1))
                    last.then_inc(ye_done, 1)

                def experts_of(t):
                    both = pe.value_load(eid[0:1, bass.ds(t, 1)], min_val=0, max_val=E * E - 1)
                    return both & (E - 1), (both >> (E - 1).bit_length()).with_bounds(min_val=0, max_val=E - 1)

                def tile(t, h, p):
                    e, e_before = experts_of(t)
                    early = t if isinstance(t, int) else ET
                    pe.wait_ge(xt_ready, t + (base + 1))
                    up(p, w11_hi, w11_lo, ps_g, e, g_done)
                    if early > 0:
                        hidden_in(t - 1, 1 - p)
                    if early != ET - 1:
                        rows_in(t + 1, h + p, 1 - p)
                    up(p, w12_hi, w12_lo, ps_v, e, v_done)
                    if early > 1:
                        down(t - 2, p, e_before)

                pe.wait_ge(slots_ready, r + 1)
                if r == 0:
                    pe.wait_ge(w2_hi_ready, W2_PIECES)
                    pe.wait_ge(lo11_ready, E)
                    pe.wait_ge(lo12_ready, E)
                else:
                    pe.wait_ge(lo_in, 32)
                rows_in(0, 0, 0)
                for t in range(3):
                    tile(t, t // 2, t % 2)
                with pe.Fori(0, (ET - 5) // 2) as h:
                    tile(h * 2 + 3, h + 1, 1)
                    tile(h * 2 + 4, h + 2, 0)
                for t in range(ET - 2, ET):
                    tile(t, t // 2, t % 2)
                hidden_in(ET - 1, (ET - 1) % 2)
                for t in range(ET - 2, ET):
                    down(t, t % 2, experts_of(t + 2)[1])

            pe.wait_ge(const_ready, 1)
            transposes(0, 0)
            transposes(1, 1)
            pe.wait_ge(s_wg, 16)
            route_chunk(0, 0, 0)
            transposes(2, 0)
            route_chunk(1, 1, 1)
            fold()
            transposes(3, 1)
            route_chunk(2, 2, 0)
            with pe.Fori(0, NCH // 2 - 2) as j:
                for b in range(2):
                    k = j * 2 + (b + 3)
                    transposes(k + 1, b)
                    route_chunk(k, k, 1 - b)
            route_chunk(NCH - 1, NCH - 1, 1)
            router(0)
            experts(0)

            def project(i, b, last=False):
                first = isinstance(i, int) and i == 0
                for jc in range(2 * DC):
                    if jc == 0:
                        pe.wait_ge(xnt_ready, i + (NCH + 1))
                    if jc == DC:
                        if not (isinstance(i, int) and i < 2):
                            ssm_in(i - 2, b)
                        if not last:
                            transposes(i + (NCH + 1), 1 - b)
                    if not first:
                        pe.wait_ge(xz_ready, i * 4 + (jc - 3))
                    for c in range(DC):
                        mm = nc.tensor.matmul(ps_p[jc][:], inw_sb[:, c, jc * P:(jc + 1) * P], xnt[b][:, c, :], start=(c == 0), stop=(c == DC - 1))
                    mm.then_inc(proj_done, 1)

            def ssm_in(c, b):
                pe.wait_ge(conv_ready, c + 1)
                pe.wait_ge(u_ready, c + 1)
                for h in range(DC):
                    last = nc.tensor.matmul(ps_u[:], wct_sb[:, h, :], conv[b][:, h, :], start=(h == 0), stop=(h == DC - 1))
                last.then_inc(u_done, 1)

            pe.wait_ge(s_attw, 48)
            transposes(NCH, 0)
            pe.wait_ge(inw_ready, 1)
            project(0, 0)
            project(1, 1)
            with pe.Fori(0, NCH // 2 - 2) as j:
                for b in range(2):
                    project(j * 2 + (b + 2), b)
            project(NCH - 2, 0)
            project(NCH - 1, 1, last=True)
            ssm_in(NCH - 2, 0)
            ssm_in(NCH - 1, 1)

            def ssm_out(i, b):
                pe.wait_ge(bwd_done, i + 2)
                if not (isinstance(i, int) and i == 0):
                    pe.wait_ge(yg_ready, i)
                for h in range(DC):
                    last = nc.tensor.matmul(ps_p[h][:], woc_sb[:, h * P:(h + 1) * P], states[:, b, :], start=True, stop=True)
                last.then_inc(y_done, 1)

            def project_out(i):
                pe.wait_ge(yg_ready, i + 1)
                if not (isinstance(i, int) and i == 0):
                    pe.wait_ge(x2_ready, i)
                for t in range(G):
                    for h in range(DC):
                        last = nc.tensor.matmul(ps_p[2 + t // 2][:, (t % 2) * D:(t % 2 + 1) * D], mix[:, h, t * P:(t + 1) * P], outw_sb[:, h, :],
                                                start=(h == 0), stop=(h == DC - 1))
                last.then_inc(o_done, 1)

            ssm_out(0, 0)
            project_out(0)
            ssm_out(1, 1)
            project_out(1)
            ssm_out(2, 0)
            transposes(2 * NCH, 0)
            with pe.Fori(0, NCH // 2 - 2) as j:
                for b in range(2):
                    i = j * 2 + (b + 2)
                    project_out(i)
                    ssm_out(i + 1, 1 - b)
                    route_chunk(j * 2 + (b + 2 * NCH), j * 2 + (b + NCH), b)
                    transposes(i + (2 * NCH - 1), 1 - b)
            for i in range(NCH - 2, NCH + 1):
                if i < NCH:
                    project_out(i)
                if i < NCH - 1:
                    ssm_out(i + 1, (i + 1) % 2)
                route_chunk(i + 2 * NCH - 2, i + NCH - 2, i % 2)
                transposes(i + 2 * NCH - 1, (i - 1) % 2)
            route_chunk(3 * NCH - 1, 2 * NCH - 1, 1)
            router(1)
            experts(1)


def kernel(**inputs):
    import numpy as np
    import concourse.bacc as bacc
    from concourse.bass_utils import run_bass_kernel_spmd

    a = {k[3:]: np.ascontiguousarray(v) for k, v in inputs.items()}
    f = {k[5:]: v for k, v in a.items() if k.startswith("attn_")}
    per_part = lambda v: v.reshape(-1, P).T
    both = lambda k: np.concatenate([f["f_" + k], f["b_" + k]]).reshape(P, 1)
    step = np.concatenate([np.broadcast_to(f["f_logdt"].reshape(1), (N,)), np.broadcast_to(f["b_logdt"].reshape(1), (N,))]).reshape(P, 1)
    cols = np.concatenate([per_part(f["norm_scale"]), per_part(f["in_b"]),
                           f["dw_w"].reshape(DC, P, 3).transpose(1, 0, 2).reshape(P, 6), per_part(f["dw_b"]), per_part(f["pw_b"]),
                           both("logA"), both("B"), both("C"), step], axis=1)
    arrays = {
        "x": f["T"].reshape(L, D), "wg": a["ffn_Wg"], "w11": a["ffn_W11"], "w12": a["ffn_W12"], "w2": a["ffn_W2"],
        "in_wt": f["in_w"].T, "pw": f["pw_w"], "wint": np.concatenate([f["f_win"], f["b_win"]], axis=0).T,
        "woutt": np.concatenate([f["f_wout"], f["b_wout"]], axis=1).T, "out_wt": f["out_w"].T,
        "out_b": f["out_b"].reshape(1, D), "cols": cols,
    }
    arrays = {k: np.ascontiguousarray(v) for k, v in arrays.items()}
    nc = bacc.Bacc("TRN2", target_bir_lowering=False, num_devices=1)
    ins = [nc.dram_tensor(k, v.shape, mybir.dt.from_np(v.dtype), kind="ExternalInput").ap() for k, v in arrays.items()]
    out = nc.dram_tensor("out_rows", [ROWS, D], F32, kind="ExternalOutput").ap()
    build(nc, *ins, out)
    r = run_bass_kernel_spmd(nc, [arrays], core_ids=[0])
    return r.results[0]["out_rows"][0:L].reshape(1, L, D)
```
